# Optimizing a Trainium2 kernel written in Bass

```python
import numpy as np
import jax
import jax.numpy as jnp

def _softmax(x, axis=-1):
    return jax.nn.softmax(x, axis=axis)

def _gelu(x):
    return jax.nn.gelu(x, approximate=True)

def _silu(x):
    return jax.nn.silu(x)

def _sigmoid(x):
    return jax.nn.sigmoid(x)

def _layernorm(x, axis=-1, eps=1e-05):
    m = jnp.mean(x, axis=axis, keepdims=True)
    v = jnp.var(x, axis=axis, keepdims=True)
    return (x - m) / jnp.sqrt(v + eps)

def _scatter_add(tgt, idx, src, axis=0):
    return tgt.at[idx].add(src)

def _segment_sum(src, seg, n):
    return jax.ops.segment_sum(src, seg, n)
kernel_name = 'mk_metaformer_d1_conv_nchw384_r2_16ce35'

def setup_inputs(seed: int=0):
    np.random.seed(seed)
    _w = jnp.asarray

    def _rec_inputs():
        import jax
        import jax.numpy as jnp
        _gk = jax.random.key(seed)
        x = -0.0001538 + 1 * jax.random.normal(jax.random.fold_in(_gk, 1), (16, 192, 32, 32), jnp.float32)
        return x
    x = _rec_inputs()

    def _L0_conv_setup():
        import jax, jax.numpy as jnp
        import numpy as np
        NUM_HEADS = 8
        EPS = 1e-12

        def _l2norm(t):
            n = jnp.sqrt(jnp.sum(t * t, axis=-1, keepdims=True))
            return t / jnp.maximum(n, EPS)
        key = jax.random.key(seed)
        ks = jax.random.split(key, 4)
        B, C, H, W = (16, 192, 32, 32)
        x = jax.random.normal(ks[0], (B, C, H, W), dtype=jnp.float32)
        temperature = jnp.ones((NUM_HEADS, 1, 1), dtype=jnp.float32)
        qkv_w = jax.random.normal(ks[1], (3 * C, C), dtype=jnp.float32) * (1.0 / np.sqrt(C))
        qkv_b = jnp.zeros((3 * C,), dtype=jnp.float32)
        proj_w = jax.random.normal(ks[2], (C, C), dtype=jnp.float32) * (1.0 / np.sqrt(C))
        proj_b = jnp.zeros((C,), dtype=jnp.float32)
        return {'x': x, 'temperature': temperature, 'qkv_w': qkv_w, 'qkv_b': qkv_b, 'proj_w': proj_w, 'proj_b': proj_b}
    _L0_conv_all = _L0_conv_setup()
    _L0_conv_in = {k: v for k, v in _L0_conv_all.items() if k in ('temperature', 'qkv_w', 'qkv_b', 'proj_w', 'proj_b')}
    del _L0_conv_all

    def _L0_ffn_setup():
        import jax, jax.numpy as jnp
        import numpy as np
        NUM_EXPERTS = 4
        TOP_K = 2
        DIM = 192
        HID = 4 * DIM
        key = jax.random.key(seed)
        ks = jax.random.split(key, 5)
        B, S = (16, 1024)
        scale_in = 1.0 / np.sqrt(DIM)
        scale_hid = 1.0 / np.sqrt(HID)
        return {'x': jax.random.normal(ks[0], (B, S, DIM), dtype=jnp.float32), 'gate_w': jax.random.normal(ks[1], (DIM, NUM_EXPERTS), dtype=jnp.float32) * scale_in, 'gate_b': jnp.zeros((NUM_EXPERTS,), dtype=jnp.float32), 'w1': jax.random.normal(ks[2], (NUM_EXPERTS, DIM, HID), dtype=jnp.float32) * scale_in, 'b1': jnp.zeros((NUM_EXPERTS, HID), dtype=jnp.float32), 'w2': jax.random.normal(ks[3], (NUM_EXPERTS, HID, DIM), dtype=jnp.float32) * scale_hid, 'b2': jnp.zeros((NUM_EXPERTS, DIM), dtype=jnp.float32)}
    _L0_ffn_all = _L0_ffn_setup()
    _L0_ffn_in = {k: v for k, v in _L0_ffn_all.items() if k in ('gate_w', 'gate_b', 'w1', 'b1', 'w2', 'b2')}
    del _L0_ffn_all
    return {'x': x, 'L0_conv_temperature': _L0_conv_in['temperature'], 'L0_conv_qkv_w': _L0_conv_in['qkv_w'], 'L0_conv_qkv_b': _L0_conv_in['qkv_b'], 'L0_conv_proj_w': _L0_conv_in['proj_w'], 'L0_conv_proj_b': _L0_conv_in['proj_b'], 'L0_ffn_gate_w': _L0_ffn_in['gate_w'], 'L0_ffn_gate_b': _L0_ffn_in['gate_b'], 'L0_ffn_w1': _L0_ffn_in['w1'], 'L0_ffn_b1': _L0_ffn_in['b1'], 'L0_ffn_w2': _L0_ffn_in['w2'], 'L0_ffn_b2': _L0_ffn_in['b2']}

def reference(x, L0_conv_temperature, L0_conv_qkv_w, L0_conv_qkv_b, L0_conv_proj_w, L0_conv_proj_b, L0_ffn_gate_w, L0_ffn_gate_b, L0_ffn_w1, L0_ffn_b1, L0_ffn_w2, L0_ffn_b2):
    import jax
    import jax.numpy as jnp

    def _L0_conv_ref(x, temperature, qkv_w, qkv_b, proj_w, proj_b):
        import jax, jax.numpy as jnp
        import numpy as np
        NUM_HEADS = 8
        EPS = 1e-12

        def _l2norm(t):
            n = jnp.sqrt(jnp.sum(t * t, axis=-1, keepdims=True))
            return t / jnp.maximum(n, EPS)
        B, C, H, W = x.shape
        nH = NUM_HEADS
        hd = C // nH
        N = H * W
        x_flat = x.reshape(B, C, N).transpose(0, 2, 1)
        qkv = x_flat @ qkv_w.T + qkv_b
        qkv = qkv.reshape(B, N, 3, nH, hd).transpose(2, 0, 3, 1, 4)
        q, k, v = (qkv[0], qkv[1], qkv[2])
        q = _l2norm(q)
        k = _l2norm(k)
        attn = jnp.einsum('bhnd,bhmd->bhnm', q, k) * temperature
        attn = jax.nn.softmax(attn, axis=-1)
        out = jnp.einsum('bhnm,bhmd->bhnd', attn, v)
        out = out.transpose(0, 2, 1, 3).reshape(B, N, C)
        out = out @ proj_w.T + proj_b
        return out.transpose(0, 2, 1).reshape(B, C, H, W)

    def _L0_ffn_ref(x, gate_w, gate_b, w1, b1, w2, b2):
        import jax, jax.numpy as jnp
        import numpy as np
        NUM_EXPERTS = 4
        TOP_K = 2
        DIM = 192
        HID = 4 * DIM
        scores = jnp.einsum('bsd,de->bse', x, gate_w) + gate_b
        probs = jax.nn.softmax(scores, axis=-1)
        topk_vals, topk_idx = jax.lax.top_k(probs, TOP_K)
        mask = jnp.sum(jax.nn.one_hot(topk_idx, NUM_EXPERTS, dtype=probs.dtype), axis=-2)
        masked = probs * mask
        masked = masked / (jnp.sum(masked, axis=-1, keepdims=True) + 1e-09)
        h = jax.nn.gelu(jnp.einsum('bsd,edh->ebsh', x, w1) + b1[:, None, None, :], approximate=False)
        y = jnp.einsum('ebsh,ehd->ebsd', h, w2) + b2[:, None, None, :]
        out = jnp.einsum('bse,ebsd->bsd', masked, y)
        return out

    def _gn(v, G=32, eps=1e-05):
        B_, C_, H_, W_ = v.shape
        g = v.reshape(B_, G, C_ // G, H_, W_)
        m = jnp.mean(g, axis=(2, 3, 4), keepdims=True)
        s = jnp.var(g, axis=(2, 3, 4), keepdims=True)
        return ((g - m) / jnp.sqrt(s + eps)).reshape(v.shape)

    def _ln_c(v, eps=1e-06):
        m = jnp.mean(v, axis=1, keepdims=True)
        s = jnp.var(v, axis=1, keepdims=True)
        return (v - m) / jnp.sqrt(s + eps)

    def _ln_t(v, eps=1e-05):
        m = jnp.mean(v, axis=-1, keepdims=True)
        s = jnp.var(v, axis=-1, keepdims=True)
        return (v - m) / jnp.sqrt(s + eps)

    def _to_tokens(v):
        B_, C_, H_, W_ = v.shape
        return v.reshape(B_, C_, H_ * W_).transpose(0, 2, 1)

    def _from_tokens(t, like):
        B_, C_, H_, W_ = like.shape
        return t.transpose(0, 2, 1).reshape(B_, C_, H_, W_)
    x = x + _L0_conv_ref(_ln_c(x), L0_conv_temperature, L0_conv_qkv_w, L0_conv_qkv_b, L0_conv_proj_w, L0_conv_proj_b)
    t = _to_tokens(x)
    t = t + _L0_ffn_ref(_ln_t(t), L0_ffn_gate_w, L0_ffn_gate_b, L0_ffn_w1, L0_ffn_b1, L0_ffn_w2, L0_ffn_b2)
    x = _from_tokens(t, x)
    return x

_drawn_inputs = setup_inputs


def setup_inputs(seed=0):
    import zlib

    import numpy as np

    out = dict(_drawn_inputs(seed))
    spreads = {'L0_conv_temperature': (1.0, 0.2),
     'L0_conv_qkv_b': (0.0, 0.1),
     'L0_conv_proj_b': (0.0, 0.1),
     'L0_ffn_gate_b': (0.0, 0.1),
     'L0_ffn_b1': (0.0, 0.1),
     'L0_ffn_b2': (0.0, 0.1)}
    factors = {}
    for name, (base, spread) in spreads.items():
        noise = np.random.default_rng([zlib.crc32(name.encode()), seed]).standard_normal(out[name].shape)
        drawn = base * np.exp(spread * noise) if base else spread * noise
        out[name] = jnp.asarray(drawn.astype(out[name].dtype))
    for name, factor in factors.items():
        out[name] = (out[name] * factor).astype(out[name].dtype)
    return out
```

```python
from contextlib import ExitStack

import concourse.bass as bass
from concourse import mybir

F32 = mybir.dt.float32
F16 = mybir.dt.float16
I32 = mybir.dt.int32
ALU = mybir.AluOpType
ACT = mybir.ActivationFunctionType
AX = mybir.AxisListType

B, C, NTOK = 16, 192, 1024
NH, HD = 8, 24
P = 128
HC = C // 2
NT = NTOK // P
HALF = 512
QKV = 3 * C
QCOLS = QKV // 2
NE, HID = 4, 4 * C
NK = HID // P
WSCALE = 64.0
EXP_RANGE = 60.0
KROWS = 4 * HD + 1
GH = NH // 2
UNITS = NH * NT
PRING = 8
QRING = 4
LN1_EPS, LN2_EPS, NORM_EPS = 1e-6, 1e-5, 1e-12
MAGIC = 1597463007.0

PRODUCTS = [(0, 0, P), (1, 1, P), (2, 2, P), (0, 3, P), (1, 4, 64)]


class Steps:

    def __init__(self, eng, sem, base=0):
        self.eng, self.sem, self.base, self.n = eng, sem, base, 0

    def mark(self, ins):
        ins.then_inc(self.sem, 1)
        self.n += 1
        return self.n

    def wait(self, n):
        self.eng.wait_ge(self.sem, self.base + n)

    def now(self, ins):
        self.wait(self.mark(ins))


def rsqrt(eng, steps, v, y, t):
    steps.now(eng.tensor_scalar(t.bitcast(I32), v.bitcast(I32), 1, None, ALU.logical_shift_right))
    steps.now(eng.tensor_scalar(y.bitcast(I32), t.bitcast(I32), -1.0, MAGIC, ALU.mult, ALU.add))
    for _ in range(3):
        steps.now(eng.scalar_tensor_tensor(t, y, -0.5, y, ALU.mult, ALU.mult))
        steps.now(eng.tensor_tensor(t, t, v, ALU.mult))
        steps.now(eng.scalar_tensor_tensor(y, t, 1.5, y, ALU.add, ALU.mult))


def mean_and_var(eng, steps, stats, mean, var, t, eps):
    steps.mark(eng.tensor_tensor(mean, stats[:, :, 1], stats[:, :, 4], ALU.add))
    steps.mark(eng.tensor_tensor(t, stats[:, :, 1], stats[:, :, 4], ALU.subtract))
    steps.now(eng.tensor_tensor(var, stats[:, :, 2], stats[:, :, 5], ALU.add))
    steps.mark(eng.tensor_scalar(mean, mean, 0.5, None, ALU.mult))
    steps.mark(eng.scalar_tensor_tensor(t, t, 0.25, t, ALU.mult, ALU.mult))
    steps.now(eng.tensor_scalar(var, var, 1.0 / C, eps, ALU.mult, ALU.add))
    steps.now(eng.tensor_tensor(var, var, t, ALU.add))


def post_order():
    out = []
    for r in range(NT + 2):
        out += [(k, r - lag) for lag, k in enumerate("abc") if 0 <= r - lag < NT]
    return out


def unit_jobs():
    jobs = {u: [("x", u)] for u in range(NT)}
    post = post_order()
    mid = [("n", 0), ("n", 1)]
    for t in range(NT):
        mid += [("u", t), ("v", t)] + ([("n", t + 2)] if t + 2 < NT else [])
    for i, j in enumerate(mid):
        jobs[12 + i] = [j]
    for t in range(NT):
        jobs[44 + 2 * t] = [("q", t), ("k", t)]
    slots = list(range(8, 12)) + sorted(list(range(36, 44)) + list(range(37, 42))) + list(range(45, 58, 2))
    for u, j in zip(slots, post, strict=True):
        jobs.setdefault(u, []).append(j)
    return jobs


JOBS = unit_jobs()
NPRE = sum(k not in "abc" for js in JOBS.values() for k, _ in js)
NPOST = sum(k in "abc" for js in JOBS.values() for k, _ in js)
PRE_STEPS = 103
POST_STEPS = 8


def job_base(img):
    if isinstance(img, int) and img <= 0:
        return NPRE * (img + 1)
    if isinstance(img, int) and img == B:
        return job_base(B - 1) + NPOST
    return 2 * NPRE + (NPRE + NPOST) * (img - 1)


def has_pre(img):
    return not isinstance(img, int) or img + 1 < B


def has_post(img):
    return not isinstance(img, int) or img >= 1


def jobs_at(img, u):
    return [(k, t) for k, t in JOBS.get(u, []) if (has_post(img) if k in "abc" else has_pre(img))]


def job_index(img, key):
    n = 0
    for u in range(UNITS):
        for j in jobs_at(img, u):
            if j == key:
                return n
            n += 1
    raise KeyError(key)


def attention_phase(nc, ctx, x, temp, qkv_w, qkv_b, proj_w, proj_b, x1_tokens):
    def sb(name, shape, dt=F32):
        return ctx.enter_context(nc.sbuf_tensor(name, shape, dt))

    def sem(name):
        return ctx.enter_context(nc.semaphore(name))

    x_img = x.rearrange("b (k c) h w -> b c k (h w)", k=2)
    x1_img = x1_tokens.rearrange("(b t p) c -> b p t c", p=P, t=NT)

    ident = sb("ident", [P, P])
    ident16 = sb("ident16", [P, P], F16)
    w_qkv = sb("w_qkv", [P, 5, QKV], F16)
    w_proj = sb("w_proj", [HC, 2, C])
    bias_qkv = sb("bias_qkv", [P, QKV])
    bias_proj = sb("bias_proj", [P, C])
    temps = sb("temps", [P, NH])
    shift = sb("shift", [P, 2, NH])
    x_in = sb("x_in", [HC, 2, NTOK])
    x_tok = sb("x_tok", [P, NT, C])
    x_res = sb("x_res", [P, 2, NT, C])
    stats = sb("stats", [P, NT, 6])
    mean = sb("mean", [P, NT])
    var = sb("var", [P, NT])
    rstd = sb("rstd", [P, NT])
    tmp8 = sb("tmp8", [P, NT])
    xn = sb("xn", [P, C])
    xn_split = sb("xn_split", [P, 2, 2 * C], F16)
    xn_t = sb("xn_t", [P, 2, 3, P], F16)
    qk = sb("qk", [P, NT, 2 * NH, HD])
    qk_sq = sb("qk_sq", [P, 2 * NH, HD])
    sumsq = sb("sumsq", [P, NT, 2 * NH])
    inv_norm = sb("inv_norm", [P, NT, 2 * NH])
    tmp128 = sb("tmp128", [P, NT * 2 * NH])
    qk_split = sb("qk_split", [P, QRING, 2 * NH, 4, HD], F16)
    v_aug = sb("v_aug", [P, 2, NT, NH, 32])
    stacks = sb("stacks", [KROWS, 2, 2, NH, NTOK], F16)
    probs = sb("probs", [P, PRING, NTOK])
    o_sb = sb("o_sb", [P, 2, 2, NTOK])
    o_norm = sb("o_norm", [P, 2, C])
    o_rec = sb("o_rec", [P, NH])
    o_t = sb("o_t", [HC, 2, 2, P])
    x1 = sb("x1", [P, NT, C])
    flat = probs[:, :, :].rearrange("p r n -> p (r n)")
    w_src = flat[0:HC, 0:6 * 2 * C].rearrange("p (j c) -> p j c", j=6)
    p_src = flat[0:HC, 2304:2304 + 2 * C].rearrange("p (j c) -> p j c", j=2)
    w_f32 = flat[:, 3072:3072 + 3 * QKV].rearrange("p (s n) -> p s n", s=3)

    ps_s = ctx.enter_context(nc.psum_tensor("ps_s", [P, 2, 2, HALF], F32))
    ps_o = ctx.enter_context(nc.psum_tensor("ps_o", [P, 2, HALF], F32))
    ps_m = ctx.enter_context(nc.psum_tensor("ps_m", [P, 2, HALF], F32))

    s_const = sem("s_const")
    s_zero = sem("s_zero")
    s_x1_free = sem("s_x1_free")
    s_wload = sem("s_wload")
    s_bload = sem("s_bload")
    s_wt = sem("s_wt")
    s_wt_free = sem("s_wt_free")
    s_setup = sem("s_setup")

    with nc.Block() as block:
        @block.sync
        def _(sp):
            wv = qkv_w.rearrange("(j r) c -> r j c", r=HC)
            sp.dma_start(w_src[:, :, 0:C], wv).then_inc(s_wload, 16)
            sp.dma_start(w_src[:, :, C:2 * C], wv).then_inc(s_wload, 16)
            sp.dma_start(p_src, proj_w.rearrange("(j r) c -> r j c", r=HC)).then_inc(s_wload, 16)
            sp.dma_start(bias_qkv[:, :], qkv_b.rearrange("(a n) -> a n", a=1).to_broadcast([P, QKV])).then_inc(s_bload, 16)
            sp.dma_start(bias_proj[:, :], proj_b.rearrange("(a n) -> a n", a=1).to_broadcast([P, C])).then_inc(s_bload, 16)
            sp.dma_start(temps[:, :], temp.rearrange("h a b -> (a b) h").to_broadcast([P, NH])).then_inc(s_bload, 16)

        @block.gpsimd
        def _(pool):
            pool.memset(ident[:, :], 0.0).then_inc(s_zero, 1)
            pool.memset(ident16[:, :], 0.0).then_inc(s_zero, 1)
            pool.wait_ge(s_zero, 2)
            for m in (ident, ident16):
                pool.affine_select(out=m[:, :], in_=m[:, :], compare_op=ALU.not_equal, fill=1.0, base=0,
                                   pattern=[[-1, P]], channel_multiplier=1).then_inc(s_const, 1)
            own = Steps(pool, s_const, 2)
            own.now(pool.memset(v_aug[:, :, :, :, HD:HD + 1], 1.0))
            own.now(pool.memset(v_aug[:, :, :, :, HD + 1:32], 0.0))
            for par in range(2):
                own.now(pool.memset(stacks[KROWS - 1:KROWS, par, 0, :, :], 1.0))
            pool.memset(x1[:, 0, 0:1], 0.0).then_inc(s_x1_free, 16)

        @block.tensor
        def _(pe):
            pe.wait_ge(s_const, 1)
            pe.wait_ge(s_wload, 48)
            n = 0
            for s, lo in ((0, 0), (1, P), (2, 64)):
                for j in range(6):
                    if n >= 2:
                        pe.wait_ge(s_wt_free, n - 1)
                    pe.transpose(ps_m[:, n % 2, 0:HC], w_src[:, j, lo:lo + P], ident[0:HC, 0:HC]).then_inc(s_wt, 1)
                    n += 1
            for k in range(2):
                for j in range(2):
                    pe.wait_ge(s_wt_free, n - 1)
                    pe.transpose(ps_m[0:HC, n % 2, 0:HC], p_src[:, j, k * HC:(k + 1) * HC],
                                 ident[0:HC, 0:HC]).then_inc(s_wt, 1)
                    n += 1

        @block.vector
        def _(dve):
            st = Steps(dve, s_setup)
            n = 0
            for s in range(3):
                for j in range(6):
                    dve.wait_ge(s_wt, n + 1)
                    dve.tensor_scalar(w_f32[:, s, j * HC:(j + 1) * HC], ps_m[:, n % 2, 0:HC], WSCALE, None,
                                      ALU.mult).then_inc(s_wt_free, 1)
                    n += 1
            for k in range(2):
                for j in range(2):
                    dve.wait_ge(s_wt, n + 1)
                    dve.tensor_copy(w_proj[:, k, j * HC:(j + 1) * HC],
                                    ps_m[0:HC, n % 2, 0:HC]).then_inc(s_wt_free, 1)
                    n += 1
            dve.wait_ge(s_wt_free, n)
            st.now(dve.tensor_copy(w_qkv[:, 0:3, :], w_f32))
            st.now(dve.tensor_tensor(w_qkv[:, 3, :], w_f32[:, 0, :], w_qkv[:, 0, :], ALU.subtract))
            st.now(dve.tensor_tensor(w_qkv[0:64, 4, :], w_f32[0:64, 1, :], w_qkv[0:64, 1, :], ALU.subtract))
            dve.wait_ge(s_bload, 48)
            st.now(dve.tensor_scalar(shift[:, 0, :], temps[:, :], -1.0, None, ALU.mult))
            st.now(dve.tensor_tensor(shift[:, 1, :], shift[:, 0, :], temps[:, :], ALU.max))
            st.now(dve.tensor_scalar(shift[:, 0, :], shift[:, 1, :], -EXP_RANGE, 0.0, ALU.add, ALU.max))
            st.now(dve.tensor_scalar(shift[:, 1, :], shift[:, 0, :], -1.0, None, ALU.mult))
            for par in range(2):
                st.now(dve.tensor_copy(stacks[KROWS - 1:KROWS, par, 1, :, :],
                                       shift[KROWS - 1:KROWS, 1, :].unsqueeze(2).to_broadcast([1, NH, NTOK])))

    s_x = sem("s_x")
    s_job = sem("s_job")
    s_job_done = sem("s_job_done")
    s_xn = sem("s_xn")
    s_qk = sem("s_qk")
    s_scores = sem("s_scores")
    s_probs = sem("s_probs")
    s_pv = sem("s_pv")
    s_o = sem("s_o")
    s_pre = sem("s_pre")
    s_post = sem("s_post")

    def sp_image(sp, img):
        if not isinstance(img, int) or img + 2 < B:
            sp.wait_ge(s_job, job_base(img) + job_index(img, ("x", NT - 1)) + 1)
            nxt = img + 2 if isinstance(img, int) else (img + 2) % B
            sp.dma_start(x_in[:, :, :], x_img[nxt]).then_inc(s_x, 16)
        if has_post(img):
            sp.wait_ge(s_job_done, job_base(img) + job_index(img, ("c", NT - 1)) + 1)
            sp.dma_start(x1_img[img - 1], x1[:, :, :]).then_inc(s_x1_free, 16)

    def scores(pe, img, par, u):
        g, m, j = u // (UNITS // 2), u % (UNITS // 2) // GH, u % GH
        h = g * GH + j
        if u == 0:
            pe.wait_ge(s_job_done, job_base(img))
        if not (isinstance(img, int) and UNITS * img + u < 2):
            pe.wait_ge(s_probs, UNITS * img + (u - 1))
        for f in range(2):
            mm = pe.matmul(ps_s[:, u % 2, f, :], stacks[:, par, 1, h, m * P:(m + 1) * P],
                           stacks[:, par, 0, h, f * HALF:(f + 1) * HALF], start=True, stop=True)
        mm.then_inc(s_scores, 1)

    def pv(pe, img, par, k):
        p, f = k // 2, k % 2
        g, m = p // (UNITS // 4), p % (UNITS // 4) // 2
        if f == 0:
            pe.wait_ge(s_probs, UNITS * img + 2 * p + 2)
        if p % (UNITS // 4) == 0 and not (isinstance(img, int) and img == 0 and g == 0):
            pe.wait_ge(s_o, 4 * img + 2 * g + f - 1)
        for u in (2 * p, 2 * p + 1):
            j = u % GH
            mm = pe.matmul(ps_o[32 * j:32 * j + 32, f, :], v_aug[:, par, m, g * GH + j, :],
                           probs[:, u % PRING, f * HALF:(f + 1) * HALF], start=(m == 0), stop=(m == NT - 1))
        mm.then_inc(s_pv, 1)

    def products(pe, out, slot, cols):
        for i, (c, w, rows) in enumerate(PRODUCTS):
            mm = pe.matmul(out, xn_t[0:rows, slot, c, :], w_qkv[0:rows, w, cols], start=(i == 0), stop=(i == 4))
        return mm

    def pe_job(pe, img, par, base, n, job):
        kind, t = job
        bank = ps_m[:, n % 2, :]
        if not (isinstance(img, int) and img == -1 and n < 2):
            pe.wait_ge(s_job_done, base + n - 1)
        tile = slice(t * P, (t + 1) * P)
        npre = NT * (img + 1)
        if kind == "x":
            if t == 0:
                pe.wait_ge(s_x, 16 * (img + 2))
            for k in range(2):
                mm = pe.transpose(bank[:, k * HC:(k + 1) * HC], x_in[:, k, tile], ident[0:HC, 0:HC])
        elif kind == "n":
            pe.wait_ge(s_xn, npre + t + 1)
            b16 = bank.bitcast(F16)
            for k in range(3):
                mm = pe.transpose(b16[:, k * P:(k + 1) * P], xn_split[:, t % 2, k * P:(k + 1) * P], ident16[:, :])
        elif kind in "uv":
            if kind == "u":
                pe.wait_ge(s_job_done, base + job_index(img, ("n", t)) + 1)
            off = QCOLS * "uv".index(kind)
            mm = products(pe, bank[:, 0:QCOLS], t % 2, slice(off, off + QCOLS))
        elif kind in "qk":
            if kind == "q":
                pe.wait_ge(s_qk, npre + t + 1)
            b16 = bank.bitcast(F16)
            for h in range(NH):
                mm = pe.transpose(b16[0:4 * HD, h * P:(h + 1) * P],
                                  qk_split[:, t % QRING, NH * "qk".index(kind) + h, :, :].rearrange("p a d -> p (a d)"),
                                  ident16[:, :])
        elif kind == "a":
            if t == 0:
                pe.wait_ge(s_o, 4 * img)
            for g in range(2):
                mm = pe.transpose(bank[:, g * P:(g + 1) * P], o_sb[:, 1 - par, g, tile], ident[:, :])
        elif kind == "b":
            pe.wait_ge(s_job_done, base + job_index(img, ("a", t)) + 1)
            for k in range(2):
                mm = pe.transpose(bank[0:HC, k * P:(k + 1) * P], o_norm[:, t % 2, k * HC:(k + 1) * HC], ident[:, :])
        else:
            pe.wait_ge(s_job_done, base + job_index(img, ("b", t)) + 1)
            for k in range(2):
                mm = pe.matmul(bank[:, 0:C], o_t[:, t % 2, k, :], w_proj[:, k, :], start=(k == 0), stop=(k == 1))
        mm.then_inc(s_job, 1)

    def pe_image(pe, img, par, attend=True):
        base, n = job_base(img), 0
        for u in range(UNITS):
            if attend:
                scores(pe, img, par, u)
            if u >= 3 and attend:
                pv(pe, img, par, u - 3)
            elif u < 3 and has_post(img):
                pv(pe, img - 1, 1 - par, UNITS - 3 + u)
            for job in jobs_at(img, u):
                pe_job(pe, img, par, base, n, job)
                n += 1

    def act_image(act, img):
        for u in range(UNITS):
            act.wait_ge(s_scores, UNITS * img + u + 1)
            if not (isinstance(img, int) and UNITS * img + u < PRING):
                act.wait_ge(s_pv, UNITS * img + 2 * ((u - PRING) // 2) + 2)
            act.activation(probs[:, u % PRING, :], ps_s[:, u % 2, :, :].rearrange("p f n -> p (f n)"),
                           ACT.Exp).then_inc(s_probs, 1)

    def take_o(dve, img, par, g, f):
        dve.wait_ge(s_pv, UNITS * img + UNITS // 2 * (g + 1) - 1 + f)
        dve.tensor_copy(o_sb[:, par, g, f * HALF:(f + 1) * HALF], ps_o[:, f, :]).then_inc(s_o, 1)

    def dve_job(dve, img, par, base, n, job, pre, post):
        kind, t = job
        bank = ps_m[:, n % 2, :]
        dve.wait_ge(s_job, base + n + 1)
        if not (isinstance(img, int) and img == -1 and n == 0):
            dve.wait_ge(s_job_done, base + n)
        nxt = 1 - par
        if kind == "x":
            dve.bn_stats(stats[:, t, :], bank[:, 0:C])
            dve.tensor_copy(x_tok[:, t, :], bank[:, 0:C]).then_inc(s_job_done, 1)
        elif kind == "n":
            dve.tensor_copy(xn_t[:, t % 2, :, :].rearrange("p k n -> p (k n)"),
                            bank.bitcast(F16)[:, 0:3 * P]).then_inc(s_job_done, 1)
            if t + 2 < NT:
                split_rows(dve, img, t + 2, pre)
        elif kind == "u":
            dve.scalar_tensor_tensor(qk[:, t, :, :].rearrange("p h d -> p (h d)")[:, 0:QCOLS], bank[:, 0:QCOLS],
                                     1.0 / WSCALE, bias_qkv[:, 0:QCOLS], ALU.mult, ALU.add).then_inc(s_job_done, 1)
        elif kind == "v":
            dve.scalar_tensor_tensor(v_aug[:, nxt, t, :, 0:HD], bank[:, HC:HC + C].rearrange("p (h d) -> p h d", d=HD),
                                     1.0 / WSCALE, bias_qkv[:, 2 * C:QKV].rearrange("p (h d) -> p h d", d=HD),
                                     ALU.mult, ALU.add)
            dve.scalar_tensor_tensor(qk[:, t, :, :].rearrange("p h d -> p (h d)")[:, QCOLS:2 * C], bank[:, 0:HC],
                                     1.0 / WSCALE, bias_qkv[:, QCOLS:2 * C], ALU.mult, ALU.add).then_inc(s_job_done, 1)
            dve.wait_ge(s_job_done, base + n + 1)
            pre.now(dve.tensor_tensor(qk_sq[:, :, :], qk[:, t, :, :], qk[:, t, :, :], ALU.mult))
            pre.now(dve.tensor_reduce(sumsq[:, t, :], qk_sq[:, :, :], AX.X, ALU.add))
        elif kind in "qk":
            dve.tensor_copy(stacks[0:4 * HD, nxt, "qk".index(kind), :, t * P:(t + 1) * P],
                            bank.bitcast(F16)[0:4 * HD, :].rearrange("p (h n) -> p h n", h=NH)).then_inc(s_job_done, 1)
        elif kind == "a":
            o = bank[:, 0:2 * P].rearrange("p (h d) -> p h d", d=32)
            post.now(dve.reciprocal(o_rec[:, :], o[:, :, HD]))
            dve.tensor_tensor(o_norm[:, t % 2, :].rearrange("p (h d) -> p h d", d=HD), o[:, :, 0:HD],
                              o_rec[:, :].unsqueeze(2).to_broadcast([P, NH, HD]), ALU.mult).then_inc(s_job_done, 1)
        elif kind == "b":
            dve.tensor_copy(o_t[:, t % 2, :, :].rearrange("p k n -> p (k n)"),
                            bank[0:HC, 0:2 * P]).then_inc(s_job_done, 1)
        else:
            if t == 0:
                dve.wait_ge(s_x1_free, 16 * img)
            dve.tensor_tensor(x1[:, t, :], bank[:, 0:C], x_res[:, nxt, t, :], ALU.add).then_inc(s_job_done, 1)
            if has_pre(img):
                dve.wait_ge(s_job_done, base + n + 1)
                residual(dve, nxt, t, pre)

    def residual(dve, nxt, t, pre):
        pre.now(dve.tensor_tensor(x_res[:, nxt, t, :], x_tok[:, t, :], bias_proj[:, :], ALU.add))

    def split_rows(dve, img, t, pre):
        if t > 0:
            dve.wait_ge(s_xn, NT * (img + 1) + t)
        pre.now(dve.tensor_scalar(xn[:, :], x_tok[:, t, :], mean[:, t:t + 1], rstd[:, t:t + 1],
                                  ALU.subtract, ALU.mult))
        pre.now(dve.tensor_copy(xn_split[:, t % 2, 0:C], xn[:, :]))
        dve.tensor_tensor(xn_split[:, t % 2, C:2 * C], xn[:, :], xn_split[:, t % 2, 0:C],
                          ALU.subtract).then_inc(s_xn, 1)

    def split_heads(dve, img, t, pre):
        s = t % QRING
        pre.now(dve.tensor_tensor(qk[:, t, :, :], qk[:, t, :, :],
                                  inv_norm[:, t, :].unsqueeze(2).to_broadcast([P, 2 * NH, HD]), ALU.mult))
        q, k = qk[:, t, 0:NH, :], qk[:, t, NH:2 * NH, :]
        q2 = q.unsqueeze(2).to_broadcast([P, NH, 2, HD])
        k2 = k.unsqueeze(2).to_broadcast([P, NH, 2, HD])
        qs, ks = qk_split[:, s, 0:NH, :, :], qk_split[:, s, NH:2 * NH, :, :]
        pre.mark(dve.tensor_copy(qs[:, :, 0:4:2, :], q2))
        pre.now(dve.tensor_copy(ks[:, :, 0:2, :], k2))
        pre.mark(dve.tensor_tensor(qs[:, :, 1:4:2, :], q2, qs[:, :, 0:4:2, :], ALU.subtract))
        dve.tensor_tensor(ks[:, :, 2:4, :], k2, ks[:, :, 0:2, :], ALU.subtract).then_inc(s_qk, 1)

    def norms_x(dve, pre, base, n):
        dve.wait_ge(s_job_done, base + n)
        mean_and_var(dve, pre, stats, mean[:, :], var[:, :], tmp8[:, :], LN1_EPS)
        rsqrt(dve, pre, var[:, :], rstd[:, :], tmp8[:, :])

    def norms_qk(dve, pre):
        pre.wait(pre.n)
        ss = sumsq[:, :, :].rearrange("p t h -> p (t h)")
        pre.now(dve.tensor_scalar(ss, ss, NORM_EPS * NORM_EPS, None, ALU.max))
        rsqrt(dve, pre, ss, inv_norm[:, :, :].rearrange("p t h -> p (t h)"), tmp128[:, :])
        pre.now(dve.tensor_tensor(inv_norm[:, :, 0:NH], inv_norm[:, :, 0:NH],
                                  temps[:, :].unsqueeze(1).to_broadcast([P, NT, NH]), ALU.mult))

    def dve_image(dve, img, par, attend=True):
        base, n = job_base(img), 0
        pre = Steps(dve, s_pre, PRE_STEPS * (img + 1))
        post = Steps(dve, s_post, POST_STEPS * (img - 1))
        if has_pre(img) and not (isinstance(img, int) and img == -1):
            dve.wait_ge(s_xn, NT * (img + 1))
            dve.wait_ge(s_qk, NT * (img + 1))
        for u in range(UNITS):
            if u in (1, 2) and has_post(img):
                take_o(dve, img - 1, 1 - par, 1, u - 1)
            if u in (33, 34) and attend:
                take_o(dve, img, par, 0, u - 33)
            for job in jobs_at(img, u):
                dve_job(dve, img, par, base, n, job, pre, post)
                n += 1
            if has_pre(img):
                if u == NT:
                    norms_x(dve, pre, base, n)
                    for t in range(2):
                        split_rows(dve, img, t, pre)
                if u == 36:
                    norms_qk(dve, pre)
                if 37 <= u < 37 + QRING:
                    split_heads(dve, img, u - 37, pre)
                if u >= 44 and (u - 44) % 2 == 0 and (u - 44) // 2 + QRING < NT:
                    split_heads(dve, img, (u - 44) // 2 + QRING, pre)
        if has_pre(img) and not has_post(img):
            for t in range(NT):
                residual(dve, 1 - par, t, pre)
        if has_post(img):
            assert post.n == POST_STEPS, post.n
        if has_pre(img):
            assert pre.n == PRE_STEPS, pre.n

    with nc.Block() as block:
        @block.sync
        def _(sp):
            sp.dma_start(x_in[:, :, :], x_img[0]).then_inc(s_x, 16)
            sp_image(sp, -1)
            sp_image(sp, 0)
            with sp.Fori(0, B // 2 - 1) as i:
                for k in range(2):
                    sp_image(sp, i * 2 + 1 + k)
            sp_image(sp, B - 1)
            sp_image(sp, B)
            sp.wait_ge(s_x1_free, 16 * (B + 1))

        @block.tensor
        def _(pe):
            pe_image(pe, -1, 1, attend=False)
            pe_image(pe, 0, 0)
            with pe.Fori(0, B // 2 - 1) as i:
                for k in range(2):
                    pe_image(pe, i * 2 + 1 + k, 1 - k)
            pe_image(pe, B - 1, 1)
            pe_image(pe, B, 0, attend=False)

        @block.scalar
        def _(act):
            act_image(act, 0)
            with act.Fori(0, B // 2 - 1) as i:
                for k in range(2):
                    act_image(act, i * 2 + 1 + k)
            act_image(act, B - 1)

        @block.vector
        def _(dve):
            dve_image(dve, -1, 1, attend=False)
            dve_image(dve, 0, 0)
            with dve.Fori(0, B // 2 - 1) as i:
                for k in range(2):
                    dve_image(dve, i * 2 + 1 + k, 1 - k)
            dve_image(dve, B - 1, 1)
            dve_image(dve, B, 0, attend=False)


BT = 4
BTOK = BT * P
NBLK = B * NTOK // BTOK
STEPS = NE * NK
LAG = 2
HBUF, HSPLIT = 3, 4
MLP_PRE_STEPS = 58
SPLIT_STEPS = 7
F_AT, N_AT, G_AT = 4, 10, 14
EXP_AT, GATE_AT = 16, 17


def mlp_jobs_at(blk, n):
    post = not isinstance(blk, int) or blk >= 1
    pre = not isinstance(blk, int) or blk + 1 < NBLK
    jobs = []
    if post and F_AT <= n < F_AT + BT:
        jobs.append(("f", n - F_AT))
    if pre and N_AT <= n < N_AT + BT:
        jobs.append(("n", n - N_AT))
    if pre and n == G_AT:
        jobs.append(("g", 0))
    return jobs


def mlp_job_base(blk):
    if isinstance(blk, int) and blk <= 0:
        return (BT + 1) * (blk + 1)
    if isinstance(blk, int) and blk == NBLK:
        return mlp_job_base(blk - 1) + BT
    return 2 * (BT + 1) + (2 * BT + 1) * (blk - 1)


def mlp_phase(nc, ctx, x1_tokens, gate_w, gate_b, w1, b1, w2, b2, out):
    def sb(name, shape, dt=F32):
        return ctx.enter_context(nc.sbuf_tensor(name, shape, dt))

    def sem(name):
        return ctx.enter_context(nc.semaphore(name))

    x1_blk = x1_tokens.rearrange("(q t p) c -> q p t c", p=P, t=BT)
    out_img = out.rearrange("b (k c) h w -> b c k (h w)", k=2)

    ident = sb("m_ident", [P, P])
    ident16 = sb("m_ident16", [P, P], F16)
    w1_sb = sb("w1_sb", [P, NE, 5, HID], F16)
    w2_sb = sb("w2_sb", [P, NE, 2, NK, C], F16)
    wg_sb = sb("wg_sb", [P, 5, NE], F16)
    bias1 = sb("bias1", [P, NE * NK])
    bias2 = sb("bias2", [P, NE, C])
    bias_g = sb("bias_g", [P, NE])
    lower = sb("lower", [P, NE, NE])
    stage1 = sb("stage1", [P, 2, 3, HID])
    stage2 = sb("stage2", [P, 2, NK, C])
    stage_g = sb("stage_g", [P, 3, NE])
    stage_b = sb("stage_b", [NE * NK, P])
    x1_in = sb("x1_in", [P, BT, C])
    stats = sb("m_stats", [P, BT, 6])
    mean = sb("m_mean", [P, BT])
    var = sb("m_var", [P, BT])
    rstd = sb("m_rstd", [P, BT])
    tmp4 = sb("m_tmp4", [P, BT])
    xn = sb("m_xn", [P, BT, C])
    xn_split = sb("m_xn_split", [P, BT, 2 * C], F16)
    xn_t = sb("m_xn_t", [P, 2, 3, BTOK], F16)
    h_f32 = sb("h_f32", [P, HBUF, BTOK])
    h_split = sb("h_split", [P, HSPLIT, 2, BTOK], F16)
    acc = sb("acc", [P, 2, BT, C])
    logits = sb("logits", [P, BT, NE])
    top = sb("top", [P, BT])
    expo = sb("expo", [P, BT, NE])
    prob = sb("prob", [P, BT, NE])
    beats = sb("beats", [P, BT, NE, NE])
    ties = sb("ties", [P, BT, NE, NE])
    rank = sb("rank", [P, BT, NE])
    total = sb("total", [P, BT])
    gates = sb("gates", [P, 2, BT, NE])
    gates_w = sb("gates_w", [P, 2, BT, NE])
    y_out = sb("y_out", [HC, 2, BTOK])

    ps_h = ctx.enter_context(nc.psum_tensor("ps_h", [P, HBUF, BTOK], F32))
    ps_y = ctx.enter_context(nc.psum_tensor("ps_y", [P, 2, 2, 512], F32))
    ps_j = ctx.enter_context(nc.psum_tensor("ps_j", [P, 512], F32))

    s_zero, s_const = sem("m_zero"), sem("m_const")
    s_wl = [sem(f"m_w1_load{e}") for e in range(2)]
    s_bl = sem("m_b_load")
    s_b1 = sem("m_b1")
    s_setup = sem("m_setup")
    s_out = sem("m_out")

    with nc.Block() as block:
        @block.sync
        def _(sp):
            for e in range(NE):
                if e >= 2:
                    sp.wait_ge(s_setup, SPLIT_STEPS * (e - 1))
                for s, (lo, hi, at) in enumerate(((0, P, 0), (P, C, 0), (64, C, 0))):
                    sp.dma_start(stage1[at:at + hi - lo, e % 2, s, :], w1[e, lo:hi, :]).then_inc(s_wl[e % 2], 16)
                sp.dma_start(stage1[64:P, e % 2, 1, :], w1[e, 0:64, :]).then_inc(s_wl[e % 2], 16)
                sp.dma_start(stage2[:, e % 2, :, :], w2[e].rearrange("(k p) c -> p k c", p=P)).then_inc(s_wl[e % 2], 16)

        @block.scalar
        def _(act):
            for s, (lo, hi) in enumerate(((0, P), (P, C), (64, C))):
                act.dma_start(stage_g[0:hi - lo, s, :], gate_w[lo:hi, :]).then_inc(s_bl, 16)
            act.dma_start(stage_g[64:P, 1, :], gate_w[0:64, :]).then_inc(s_bl, 16)
            act.dma_start(stage_b[:, :], b1.rearrange("e (k p) -> (e k) p", p=P)).then_inc(s_bl, 16)
            act.dma_start(bias2[:, :, :], b2.rearrange("(a e) c -> a e c", a=1).to_broadcast([P, NE, C])).then_inc(s_bl, 16)
            act.dma_start(bias_g[:, :], gate_b.rearrange("(a e) -> a e", a=1).to_broadcast([P, NE])).then_inc(s_bl, 16)

        @block.gpsimd
        def _(pool):
            pool.memset(ident[:, :], 0.0).then_inc(s_zero, 1)
            pool.memset(ident16[:, :], 0.0).then_inc(s_zero, 1)
            pool.memset(lower[:, :, :], 0.0).then_inc(s_zero, 1)
            pool.wait_ge(s_zero, 3)
            for m in (ident, ident16):
                pool.affine_select(out=m[:, :], in_=m[:, :], compare_op=ALU.not_equal, fill=1.0, base=0,
                                   pattern=[[-1, P]], channel_multiplier=1).then_inc(s_const, 1)
            own = Steps(pool, s_const, 2)
            for i in range(1, NE):
                own.now(pool.memset(lower[:, i, 0:i], 1.0))
            pool.memset(y_out[:, 0, 0:1], 0.0).then_inc(s_out, 16)

        @block.tensor
        def _(pe):
            pe.wait_ge(s_const, 1)
            pe.wait_ge(s_bl, 16 * 7)
            pe.transpose(ps_j[:, 0:NE * NK], stage_b[:, :], ident[0:NE * NK, 0:NE * NK]).then_inc(s_b1, 1)

        @block.vector
        def _(dve):
            st = Steps(dve, s_setup)

            def split(src, parts, lows):
                st.now(dve.tensor_scalar(src, src, WSCALE, None, ALU.mult))
                st.now(dve.tensor_copy(parts, src))
                for a, hi, lo in lows:
                    st.mark(dve.tensor_tensor(lo, a, hi, ALU.subtract))
                st.wait(st.n)

            for e in range(NE):
                dve.wait_ge(s_wl[e % 2], 80 * (e // 2 + 1))
                a = stage1[:, e % 2, :, :]
                split(a, w1_sb[:, e, 0:3, :], [(a[:, 0, :], w1_sb[:, e, 0, :], w1_sb[:, e, 3, :]),
                                               (a[0:64, 1, :], w1_sb[0:64, e, 1, :], w1_sb[0:64, e, 4, :])])
                a = stage2[:, e % 2, :, :]
                split(a, w2_sb[:, e, 0, :, :], [(a, w2_sb[:, e, 0, :, :], w2_sb[:, e, 1, :, :])])
            dve.wait_ge(s_bl, 16 * 7)
            a = stage_g[:, :, :]
            split(a, wg_sb[:, 0:3, :], [(a[:, 0, :], wg_sb[:, 0, :], wg_sb[:, 3, :]),
                                        (a[0:64, 1, :], wg_sb[0:64, 1, :], wg_sb[0:64, 4, :])])
            dve.wait_ge(s_b1, 1)
            dve.tensor_copy(bias1[:, :], ps_j[:, 0:NE * NK])

    s_x1 = sem("m_x1")
    s_job = sem("m_job")
    s_job_done = sem("m_job_done")
    s_xn = sem("m_xn")
    s_w1 = sem("m_h")
    s_gelu = sem("m_gelu")
    s_h = sem("m_hsplit")
    s_w2 = sem("m_y")
    s_acc = sem("m_acc")
    s_logit = sem("m_logit")
    s_exp = sem("m_exp")
    s_acc0 = sem("m_acc0")
    s_pre = sem("m_pre")
    s_own = sem("m_own")

    def first(blk):
        return isinstance(blk, int) and blk == -1

    def sp_block(sp, blk, img, half):
        if not isinstance(blk, int) or blk >= 1:
            sp.wait_ge(s_job_done, mlp_job_base(blk) + BT)
            sp.dma_start(out_img[img][:, :, half * BTOK:(half + 1) * BTOK], y_out[:, :, :]).then_inc(s_out, 16)
        if not isinstance(blk, int) or blk + 2 < NBLK:
            nxt = blk + 2 if isinstance(blk, int) else (blk + 2) % NBLK
            sp.wait_ge(s_acc0, blk + 2)
            sp.dma_start(x1_in[:, :, :], x1_blk[nxt]).then_inc(s_x1, 16)

    def first_product(pe, blk, par, n):
        e, k = n // NK, n % NK
        if n == 0:
            pe.wait_ge(s_job_done, mlp_job_base(blk))
        if not (isinstance(blk, int) and STEPS * blk + n < HBUF):
            pe.wait_ge(s_gelu, STEPS * blk + n - HBUF + 1)
        for i, (c, w, rows) in enumerate(PRODUCTS):
            mm = pe.matmul(ps_h[:, n % HBUF, :], w1_sb[0:rows, e, w, k * P:(k + 1) * P], xn_t[0:rows, par, c, :],
                           start=(i == 0), stop=(i == 4))
        mm.then_inc(s_w1, 1)

    def second_product(pe, blk, n):
        e, k = n // NK, n % NK
        pe.wait_ge(s_h, STEPS * blk + n + 1)
        if k == 0 and not (isinstance(blk, int) and NE * blk + e < 2):
            pe.wait_ge(s_acc, NE * blk + e - 1)
        for t in range(BT):
            y = ps_y[:, e % 2, t // 2, (t % 2) * C:(t % 2 + 1) * C]
            tok = slice(t * P, (t + 1) * P)
            for i, (hp, wp) in enumerate(((0, 0), (0, 1), (1, 0))):
                mm = pe.matmul(y, h_split[:, n % HSPLIT, hp, tok], w2_sb[:, e, wp, k, :],
                               start=(k == 0 and i == 0 and t % 2 == 0), stop=(k == NK - 1 and i == 2),
                               skip_group_check=True)
        mm.then_inc(s_w2, 1)

    def pe_mlp_job(pe, blk, par, base, j, job):
        kind, t = job
        if not (first(blk) and j == 0):
            pe.wait_ge(s_job_done, base + j)
        if kind == "f":
            if t == 0:
                pe.wait_ge(s_acc, NE * blk)
            for k in range(2):
                mm = pe.transpose(ps_j[0:HC, k * P:(k + 1) * P], acc[:, 1 - par, t, k * HC:(k + 1) * HC], ident[:, :])
        elif kind == "n":
            if t == 0:
                pe.wait_ge(s_xn, blk + 2)
            b16 = ps_j[:, :].bitcast(F16)
            for k in range(3):
                mm = pe.transpose(b16[:, k * P:(k + 1) * P], xn_split[:, t, k * P:(k + 1) * P], ident16[:, :])
        else:
            for t in range(BT):
                for i, (c, w, rows) in enumerate(PRODUCTS):
                    mm = pe.matmul(ps_j[:, t * NE:(t + 1) * NE], xn_t[0:rows, 1 - par, c, t * P:(t + 1) * P],
                                   wg_sb[0:rows, w, :], start=(i == 0), stop=(i == 4))
        mm.then_inc(s_job, 1)

    def pe_block(pe, blk, par, main=True):
        base, j = mlp_job_base(blk), 0
        for n in range(STEPS):
            if main:
                first_product(pe, blk, par, n)
            if n >= LAG and main:
                second_product(pe, blk, n - LAG)
            elif n < LAG and (not isinstance(blk, int) or blk >= 1):
                second_product(pe, blk - 1, STEPS - LAG + n)
            for job in mlp_jobs_at(blk, n):
                pe_mlp_job(pe, blk, par, base, j, job)
                j += 1

    def act_block(act, blk, main=True):
        for n in range(STEPS):
            if main:
                act.wait_ge(s_w1, STEPS * blk + n + 1)
                if not (isinstance(blk, int) and STEPS * blk + n < HBUF):
                    act.wait_ge(s_h, STEPS * blk + n - HBUF + 1)
                act.activation(h_f32[:, n % HBUF, :], ps_h[:, n % HBUF, :], ACT.Gelu, bias=bias1[:, n:n + 1],
                               scale=1.0 / WSCALE).then_inc(s_gelu, 1)
            if n == EXP_AT and (not isinstance(blk, int) or blk + 1 < NBLK):
                act.wait_ge(s_logit, blk + 2)
                act.activation(expo[:, :, :], logits[:, :, :], ACT.Exp).then_inc(s_exp, 1)

    def split_hidden(dve, blk, n, own):
        dve.wait_ge(s_gelu, STEPS * blk + n + 1)
        if not (isinstance(blk, int) and STEPS * blk + n < HSPLIT):
            dve.wait_ge(s_w2, STEPS * blk + n - HSPLIT + 1)
        own.now(dve.tensor_copy(h_split[:, n % HSPLIT, 0, :], h_f32[:, n % HBUF, :]))
        dve.tensor_tensor(h_split[:, n % HSPLIT, 1, :], h_f32[:, n % HBUF, :], h_split[:, n % HSPLIT, 0, :],
                          ALU.subtract).then_inc(s_h, 1)

    def add_expert(dve, blk, par, e, own):
        dve.wait_ge(s_w2, STEPS * blk + (e + 1) * NK)
        for t in range(BT):
            ins = dve.scalar_tensor_tensor(acc[:, par, t, :], ps_y[:, e % 2, t // 2, (t % 2) * C:(t % 2 + 1) * C],
                                           gates_w[:, par, t, e:e + 1], acc[:, par, t, :], ALU.mult, ALU.add)
            if t < BT - 1:
                own.mark(ins)
        ins.then_inc(s_acc, 1)
        dve.wait_ge(s_acc, NE * blk + e + 1)

    def mlp_dve_job(dve, blk, par, base, j, job, pre):
        kind, t = job
        dve.wait_ge(s_job, base + j + 1)
        if not (first(blk) and j == 0):
            dve.wait_ge(s_job_done, base + j)
        if kind == "f":
            if t == 0:
                dve.wait_ge(s_out, 16 * blk)
            dve.tensor_copy(y_out[:, :, t * P:(t + 1) * P],
                            ps_j[0:HC, 0:2 * P].rearrange("p (k n) -> p k n", k=2)).then_inc(s_job_done, 1)
        elif kind == "n":
            dve.tensor_copy(xn_t[:, 1 - par, :, t * P:(t + 1) * P],
                            ps_j[:, :].bitcast(F16)[:, 0:3 * P].rearrange("p (k n) -> p k n", k=3)).then_inc(s_job_done, 1)
        else:
            dve.scalar_tensor_tensor(logits[:, :, :], ps_j[:, 0:BT * NE].rearrange("p (t e) -> p t e", e=NE),
                                     1.0 / WSCALE, bias_g[:, :].unsqueeze(1).to_broadcast([P, BT, NE]),
                                     ALU.mult, ALU.add).then_inc(s_job_done, 1)
            dve.wait_ge(s_job_done, base + j + 1)
            pre.now(dve.tensor_reduce(top[:, :], logits[:, :, :], AX.X, ALU.max))
            dve.tensor_tensor(logits[:, :, :], logits[:, :, :], top[:, :].unsqueeze(2).to_broadcast([P, BT, NE]),
                              ALU.subtract).then_inc(s_logit, 1)

    def gate_weights(dve, blk, nxt, pre):
        dve.wait_ge(s_exp, blk + 2)
        dve.wait_ge(s_logit, blk + 2)
        bc = lambda v: v.unsqueeze(2).to_broadcast([P, BT, NE])
        pre.now(dve.tensor_reduce(total[:, :], expo[:, :, :], AX.X, ALU.add))
        pre.now(dve.reciprocal(total[:, :], total[:, :]))
        pre.now(dve.tensor_tensor(prob[:, :, :], expo[:, :, :], bc(total[:, :]), ALU.mult))
        p_i = prob[:, :, :].unsqueeze(3).to_broadcast([P, BT, NE, NE])
        p_j = prob[:, :, :].unsqueeze(2).to_broadcast([P, BT, NE, NE])
        pre.mark(dve.tensor_tensor(beats[:, :, :, :], p_j, p_i, ALU.is_gt))
        pre.now(dve.tensor_tensor(ties[:, :, :, :], p_j, p_i, ALU.is_equal))
        pre.now(dve.tensor_tensor(ties[:, :, :, :], ties[:, :, :, :],
                                  lower[:, :, :].unsqueeze(1).to_broadcast([P, BT, NE, NE]), ALU.mult))
        pre.now(dve.tensor_tensor(beats[:, :, :, :], beats[:, :, :, :], ties[:, :, :, :], ALU.add))
        pre.now(dve.tensor_reduce(rank[:, :, :], beats[:, :, :, :], AX.X, ALU.add))
        pre.now(dve.tensor_scalar(rank[:, :, :], rank[:, :, :], 2.0, None, ALU.is_lt))
        pre.now(dve.tensor_tensor(prob[:, :, :], prob[:, :, :], rank[:, :, :], ALU.mult))
        pre.now(dve.tensor_reduce(total[:, :], prob[:, :, :], AX.X, ALU.add))
        pre.now(dve.tensor_scalar(total[:, :], total[:, :], 1e-9, None, ALU.add))
        pre.now(dve.reciprocal(total[:, :], total[:, :]))
        pre.now(dve.tensor_tensor(gates[:, nxt, :, :], prob[:, :, :], bc(total[:, :]), ALU.mult))
        pre.now(dve.tensor_scalar(gates_w[:, nxt, :, :], gates[:, nxt, :, :], 1.0 / WSCALE, None, ALU.mult))

    def start_acc(dve, blk, nxt, t, pre):
        src = x1_in[:, t, :]
        for e in range(NE):
            ins = dve.scalar_tensor_tensor(acc[:, nxt, t, :], bias2[:, e, :], gates[:, nxt, t, e:e + 1], src,
                                           ALU.mult, ALU.add)
            src = acc[:, nxt, t, :]
            if t < BT - 1 or e < NE - 1:
                pre.now(ins)
        if t == BT - 1:
            ins.then_inc(s_acc0, 1)
            dve.wait_ge(s_acc0, blk + 2)

    def dve_block(dve, blk, par, main=True):
        base, j = mlp_job_base(blk), 0
        has_pre = not isinstance(blk, int) or blk + 1 < NBLK
        has_post = not isinstance(blk, int) or blk >= 1
        nxt = 1 - par
        pre = Steps(dve, s_pre, MLP_PRE_STEPS * (blk + 1))
        own = Steps(dve, s_own, (STEPS + NE * (BT - 1)) * blk)
        if has_post:
            own.base = own.base - (BT - 1)
        for n in range(STEPS):
            if main:
                split_hidden(dve, blk, n, own)
            if n == 2 and has_post:
                add_expert(dve, blk - 1, nxt, NE - 1, own)
            if main and n in (8, 14, 20):
                add_expert(dve, blk, par, (n - 8) // NK, own)
            if has_pre:
                if n == 3:
                    dve.wait_ge(s_x1, 16 * (blk + 2))
                    for t in range(BT):
                        pre.mark(dve.bn_stats(stats[:, t, :], x1_in[:, t, :]))
                    pre.wait(pre.n)
                if n == 4:
                    mean_and_var(dve, pre, stats, mean[:, :], var[:, :], tmp4[:, :], LN2_EPS)
                if n == 5:
                    rsqrt(dve, pre, var[:, :], rstd[:, :], tmp4[:, :])
                if n == 6:
                    if not first(blk):
                        dve.wait_ge(s_xn, blk + 1)
                    for t in range(BT):
                        pre.mark(dve.tensor_scalar(xn[:, t, :], x1_in[:, t, :], mean[:, t:t + 1],
                                                   rstd[:, t:t + 1], ALU.subtract, ALU.mult))
                    pre.wait(pre.n)
                if n == 7:
                    pre.now(dve.tensor_copy(xn_split[:, :, 0:C], xn[:, :, :]))
                if n == 9:
                    dve.tensor_tensor(xn_split[:, :, C:2 * C], xn[:, :, :], xn_split[:, :, 0:C],
                                      ALU.subtract).then_inc(s_xn, 1)
            for job in mlp_jobs_at(blk, n):
                mlp_dve_job(dve, blk, par, base, j, job, pre)
                j += 1
            if has_pre:
                if n == GATE_AT:
                    gate_weights(dve, blk, nxt, pre)
                if n in (18, 19, 21, 22):
                    start_acc(dve, blk, nxt, (18, 19, 21, 22).index(n), pre)
        if has_pre:
            assert pre.n == MLP_PRE_STEPS, pre.n

    with nc.Block() as block:
        @block.sync
        def _(sp):
            sp.dma_start(x1_in[:, :, :], x1_blk[0]).then_inc(s_x1, 16)
            sp_block(sp, -1, 0, 0)
            sp_block(sp, 0, 0, 0)
            with sp.Fori(0, NBLK // 2 - 1) as i:
                for k in range(2):
                    sp_block(sp, i * 2 + 1 + k, i, k)
            sp_block(sp, NBLK - 1, B - 1, 0)
            sp_block(sp, NBLK, B - 1, 1)
            sp.wait_ge(s_out, 16 * (NBLK + 1))

        @block.tensor
        def _(pe):
            pe_block(pe, -1, 1, main=False)
            pe_block(pe, 0, 0)
            with pe.Fori(0, NBLK // 2 - 1) as i:
                for k in range(2):
                    pe_block(pe, i * 2 + 1 + k, 1 - k)
            pe_block(pe, NBLK - 1, 1)
            pe_block(pe, NBLK, 0, main=False)

        @block.scalar
        def _(act):
            act_block(act, -1, main=False)
            act_block(act, 0)
            with act.Fori(0, NBLK // 2 - 1) as i:
                for k in range(2):
                    act_block(act, i * 2 + 1 + k)
            act_block(act, NBLK - 1)

        @block.vector
        def _(dve):
            dve_block(dve, -1, 1, main=False)
            dve_block(dve, 0, 0)
            with dve.Fori(0, NBLK // 2 - 1) as i:
                for k in range(2):
                    dve_block(dve, i * 2 + 1 + k, 1 - k)
            dve_block(dve, NBLK - 1, 1)
            dve_block(dve, NBLK, 0, main=False)


_INS = ['x', 'L0_conv_temperature', 'L0_conv_qkv_w', 'L0_conv_qkv_b', 'L0_conv_proj_w', 'L0_conv_proj_b',
        'L0_ffn_gate_w', 'L0_ffn_gate_b', 'L0_ffn_w1', 'L0_ffn_b1', 'L0_ffn_w2', 'L0_ffn_b2']
_OUTS = [((B, C, 32, 32), 'float32')]


def metaformer_block(nc, x, temp, qkv_w, qkv_b, proj_w, proj_b, gate_w, gate_b, w1, b1, w2, b2, out, x1_tokens=None):
    if x1_tokens is None:
        x1_tokens = nc.dram_tensor("x1_tokens", [B * NTOK, C], F32, kind="Internal").ap()
    with ExitStack() as ctx:
        attention_phase(nc, ctx, x, temp, qkv_w, qkv_b, proj_w, proj_b, x1_tokens)
    with ExitStack() as ctx:
        mlp_phase(nc, ctx, x1_tokens, gate_w, gate_b, w1, b1, w2, b2, out)


def kernel(**inputs):
    import numpy as _np
    import concourse.bacc as _bacc
    from concourse.bass_utils import run_bass_kernel_spmd as _run

    nc = _bacc.Bacc("TRN2", target_bir_lowering=False, num_devices=1)
    arrays, args = {}, []
    for name in _INS:
        a = _np.ascontiguousarray(inputs[name])
        arrays[f"in_{name}_dram"] = a
        args.append(nc.dram_tensor(f"in_{name}_dram", a.shape, mybir.dt.from_np(a.dtype), kind="ExternalInput").ap())
    for i, (shape, dtype) in enumerate(_OUTS):
        dt = mybir.dt.from_np(_np.dtype(dtype))
        args.append(nc.dram_tensor(f"out_{i}_dram", shape, dt, kind="ExternalOutput").ap())
    metaformer_block(nc, *args)
    r = _run(nc, [arrays], core_ids=[0])
    return r.results[0]["out_0_dram"]
```

```python
from contextlib import ExitStack

import concourse.bass as bass
from concourse import mybir

F32 = mybir.dt.float32
F16 = mybir.dt.float16
I32 = mybir.dt.int32
ALU = mybir.AluOpType
ACT = mybir.ActivationFunctionType
AX = mybir.AxisListType

B, C, NTOK = 16, 192, 1024
NH, HD = 8, 24
P = 128
HC = C // 2
NT = NTOK // P
HALF = 512
QKV = 3 * C
QCOLS = QKV // 2
NE, HID = 4, 4 * C
NK = HID // P
WSCALE = 64.0
EXP_RANGE = 60.0
KROWS = 4 * HD
GH = NH // 2
UNITS = NH * NT
PRING = 8
QRING = 2
LN1_EPS, LN2_EPS, NORM_EPS = 1e-6, 1e-5, 1e-12
MAGIC = 1597463007.0

PRODUCTS = [(0, 0, P), (1, 1, P), (2, 2, P), (0, 3, P), (1, 4, 64)]


class Steps:

    def __init__(self, eng, sem, base=0):
        self.eng, self.sem, self.base, self.n = eng, sem, base, 0

    def mark(self, ins):
        ins.then_inc(self.sem, 1)
        self.n += 1
        return self.n

    def wait(self, n):
        self.eng.wait_ge(self.sem, self.base + n)

    def now(self, ins):
        self.wait(self.mark(ins))


def rsqrt(eng, steps, v, y, t, part):
    if part == 0:
        rsqrt_guess(eng, steps, v, y, t)
    steps.now(eng.scalar_tensor_tensor(t, y, -0.5, y, ALU.mult, ALU.mult))
    steps.now(eng.tensor_tensor(t, t, v, ALU.mult))
    steps.now(eng.scalar_tensor_tensor(y, t, 1.5, y, ALU.add, ALU.mult))


def rsqrt_guess(eng, steps, v, y, t):
    steps.now(eng.tensor_scalar(t.bitcast(I32), v.bitcast(I32), 1, None, ALU.logical_shift_right))
    steps.now(eng.tensor_scalar(y.bitcast(I32), t.bitcast(I32), -1.0, MAGIC, ALU.mult, ALU.add))


def mean_and_var(eng, steps, stats, mean, var, t, eps, done=None):
    steps.mark(eng.tensor_tensor(mean, stats[:, :, 1], stats[:, :, 4], ALU.add))
    steps.mark(eng.tensor_tensor(t, stats[:, :, 1], stats[:, :, 4], ALU.subtract))
    steps.now(eng.tensor_tensor(var, stats[:, :, 2], stats[:, :, 5], ALU.add))
    steps.mark(eng.tensor_scalar(mean, mean, 0.5, 0.0, ALU.mult, ALU.add))
    steps.mark(eng.tensor_scalar(t, t, 0.5, 0.0, ALU.mult, ALU.add))
    steps.now(eng.tensor_scalar(var, var, 1.0 / C, eps, ALU.mult, ALU.add))
    steps.now(eng.tensor_tensor(t, t, t, ALU.mult))
    last = eng.tensor_tensor(var, var, t, ALU.add)
    if done is None:
        steps.now(last)
    else:
        last.then_inc(done, 1)


def post_order():
    out = []
    for r in range(NT + 2):
        out += [(k, r - lag) for lag, k in enumerate("abc") if 0 <= r - lag < NT]
    return out


ROUND0, ROUND = 13, 5
POST_SLOTS = [(1, 3, 4), (1, 3, 4)] + [(3, 4)] * (NT - 1)


def unit_jobs():
    post = iter(post_order())
    jobs = {u: [("x", u)] for u in range(NT)}
    jobs.update({u: [next(post)] for u in range(NT, ROUND0 - 1)})
    jobs[ROUND0 - 1] = [("n", 0)]
    for r in range(NT + 2):
        u = ROUND0 + ROUND * r
        jobs.update({u + v: [] for v in range(ROUND)})
        if r < NT:
            jobs[u].append(("u", r))
            jobs[u + 1].append(("v", r))
        if r >= 2:
            jobs[u].append(("q", r - 2))
            jobs[u + 2].append(("k", r - 2))
        if r + 1 < NT:
            jobs[u + 2].append(("n", r + 1))
        for v in POST_SLOTS[r] if r <= NT else ():
            jobs[u + v].append(next(post))
    assert next(post, None) is None and jobs[ROUND0 + ROUND * (NT + 1) + 2][-1] == ("k", NT - 1)
    return jobs


JOBS = unit_jobs()
ON_SCALAR = "qkn"
PRE_STEPS = 63
POST_STEPS = 8


def has_pre(img):
    return not isinstance(img, int) or img + 1 < B


def has_post(img):
    return not isinstance(img, int) or img >= 1


def jobs_at(img, u):
    return [(k, t) for k, t in JOBS.get(u, []) if (has_post(img) if k in "abc" else has_pre(img))]


def jobs_of(img):
    return [j for u in range(UNITS) for j in jobs_at(img, u)]


def count(jobs, scalar=None):
    return sum(scalar is None or (k in ON_SCALAR) == scalar for k, _ in jobs)


def jobs_before(img, scalar=None):
    if isinstance(img, int) and img <= 1 or isinstance(img, int) and img == B:
        return sum(count(jobs_of(i), scalar) for i in range(-1, img))
    return jobs_before(1, scalar) + count(jobs_of(2), scalar) * (img - 1)


def attention_phase(nc, ctx, x, temp, qkv_w, qkv_b, proj_w, proj_b, x1_tokens):
    def sb(name, shape, dt=F32):
        return ctx.enter_context(nc.sbuf_tensor(name, shape, dt))

    def sem(name):
        return ctx.enter_context(nc.semaphore(name))

    x_img = x.rearrange("b (k c) h w -> b c k (h w)", k=2)
    x1_img = x1_tokens.rearrange("(b t p) c -> b p t c", p=P, t=NT)

    ident = sb("ident", [P, P])
    ident16 = sb("ident16", [P, P], F16)
    w_qkv = sb("w_qkv", [P, 5, QKV], F16)
    w_proj = sb("w_proj", [HC, 2, C])
    bias_qkv = sb("bias_qkv", [P, QKV])
    bias_proj = sb("bias_proj", [P, C])
    temps = sb("temps", [P, NH])
    shift = sb("shift", [P, 2, NH])
    x_in = sb("x_in", [HC, 2, NTOK])
    x_tok = sb("x_tok", [P, NT, C])
    x_res = sb("x_res", [P, 2, NT, C])
    stats = sb("stats", [P, NT, 6])
    mean = sb("mean", [P, NT])
    var = sb("var", [P, NT])
    rstd = sb("rstd", [P, NT])
    tmp8 = sb("tmp8", [P, NT])
    xn = sb("xn", [P, C])
    xn_split = sb("xn_split", [P, 2, 2 * C], F16)
    xn_t = sb("xn_t", [P, 2, 3, P], F16)
    qk = sb("qk", [P, NT, 2 * NH, HD])
    qk_sq = sb("qk_sq", [P, 2 * NH, HD])
    sumsq = sb("sumsq", [P, NT, 2 * NH])
    inv_norm = sb("inv_norm", [P, NT, 2 * NH])
    minus_half = sb("minus_half", [P, 2 * NH])
    qk_split = sb("qk_split", [P, QRING, 2 * NH, 4, HD], F16)
    v_aug = sb("v_aug", [P, 2, NT, NH, 32])
    stacks = sb("stacks", [KROWS, 2, 2, NH, NTOK], F16)
    probs = sb("probs", [P, PRING, NTOK])
    o_sb = sb("o_sb", [P, 2, 2, NTOK])
    o_norm = sb("o_norm", [P, 2, C])
    o_rec = sb("o_rec", [P, NH])
    o_t = sb("o_t", [HC, 2, 2, P])
    x1 = sb("x1", [P, NT, C])
    flat = probs[:, :, :].rearrange("p r n -> p (r n)")
    w_src = flat[0:HC, 0:6 * 2 * C].rearrange("p (j c) -> p j c", j=6)
    p_src = flat[0:HC, 2304:2304 + 2 * C].rearrange("p (j c) -> p j c", j=2)
    w_f32 = flat[:, 3072:3072 + 3 * QKV].rearrange("p (s n) -> p s n", s=3)

    ps_s = ctx.enter_context(nc.psum_tensor("ps_s", [P, 2, 2, HALF], F32))
    ps_o = ctx.enter_context(nc.psum_tensor("ps_o", [P, 2, HALF], F32))
    ps_m = ctx.enter_context(nc.psum_tensor("ps_m", [P, 2, HALF], F32))

    s_const = sem("s_const")
    s_zero = sem("s_zero")
    s_x1_free = sem("s_x1_free")
    s_wload = sem("s_wload")
    s_bload = sem("s_bload")
    s_wt = sem("s_wt")
    s_wt_free = sem("s_wt_free")
    s_setup = sem("s_setup")

    with nc.Block() as block:
        @block.sync
        def _(sp):
            wv = qkv_w.rearrange("(j r) c -> r j c", r=HC)
            sp.dma_start(w_src[:, :, 0:C], wv).then_inc(s_wload, 16)
            sp.dma_start(w_src[:, :, C:2 * C], wv).then_inc(s_wload, 16)
            sp.dma_start(p_src, proj_w.rearrange("(j r) c -> r j c", r=HC)).then_inc(s_wload, 16)
            sp.dma_start(bias_qkv[:, :], qkv_b.rearrange("(a n) -> a n", a=1).to_broadcast([P, QKV])).then_inc(s_bload, 16)
            sp.dma_start(bias_proj[:, :], proj_b.rearrange("(a n) -> a n", a=1).to_broadcast([P, C])).then_inc(s_bload, 16)
            sp.dma_start(temps[:, :], temp.rearrange("h a b -> (a b) h").to_broadcast([P, NH])).then_inc(s_bload, 16)

        @block.gpsimd
        def _(pool):
            pool.memset(ident[:, :], 0.0).then_inc(s_zero, 1)
            pool.memset(ident16[:, :], 0.0).then_inc(s_zero, 1)
            pool.wait_ge(s_zero, 2)
            for m in (ident, ident16):
                pool.affine_select(out=m[:, :], in_=m[:, :], compare_op=ALU.not_equal, fill=1.0, base=0,
                                   pattern=[[-1, P]], channel_multiplier=1).then_inc(s_const, 1)
            own = Steps(pool, s_const, 2)
            own.now(pool.memset(v_aug[:, :, :, :, HD:HD + 1], 1.0))
            own.now(pool.memset(v_aug[:, :, :, :, HD + 1:32], 0.0))
            pool.memset(x1[:, 0, 0:1], 0.0).then_inc(s_x1_free, 16)

        @block.tensor
        def _(pe):
            pe.wait_ge(s_const, 1)
            pe.wait_ge(s_wload, 48)
            n = 0
            for s, lo in ((0, 0), (1, P), (2, 64)):
                for j in range(6):
                    if n >= 2:
                        pe.wait_ge(s_wt_free, n - 1)
                    pe.transpose(ps_m[:, n % 2, 0:HC], w_src[:, j, lo:lo + P], ident[0:HC, 0:HC]).then_inc(s_wt, 1)
                    n += 1
            for k in range(2):
                for j in range(2):
                    pe.wait_ge(s_wt_free, n - 1)
                    pe.transpose(ps_m[0:HC, n % 2, 0:HC], p_src[:, j, k * HC:(k + 1) * HC],
                                 ident[0:HC, 0:HC]).then_inc(s_wt, 1)
                    n += 1

        @block.vector
        def _(dve):
            st = Steps(dve, s_setup)
            n = 0
            for s in range(3):
                for j in range(6):
                    dve.wait_ge(s_wt, n + 1)
                    dve.tensor_scalar(w_f32[:, s, j * HC:(j + 1) * HC], ps_m[:, n % 2, 0:HC], WSCALE, None,
                                      ALU.mult).then_inc(s_wt_free, 1)
                    n += 1
            for k in range(2):
                for j in range(2):
                    dve.wait_ge(s_wt, n + 1)
                    dve.tensor_copy(w_proj[:, k, j * HC:(j + 1) * HC],
                                    ps_m[0:HC, n % 2, 0:HC]).then_inc(s_wt_free, 1)
                    n += 1
            dve.wait_ge(s_wt_free, n)
            st.now(dve.tensor_copy(w_qkv[:, 0:3, :], w_f32))
            st.now(dve.tensor_tensor(w_qkv[:, 3, :], w_f32[:, 0, :], w_qkv[:, 0, :], ALU.subtract))
            st.now(dve.tensor_tensor(w_qkv[0:64, 4, :], w_f32[0:64, 1, :], w_qkv[0:64, 1, :], ALU.subtract))
            dve.wait_ge(s_bload, 48)
            st.now(dve.memset(minus_half[:, :], -0.5))
            st.now(dve.tensor_scalar(shift[:, 0, :], temps[:, :], -1.0, None, ALU.mult))
            st.now(dve.tensor_tensor(shift[:, 1, :], shift[:, 0, :], temps[:, :], ALU.max))
            st.now(dve.tensor_scalar(shift[:, 0, :], shift[:, 1, :], -EXP_RANGE, 0.0, ALU.add, ALU.max))
            st.now(dve.tensor_scalar(shift[:, 1, :], shift[:, 0, :], -1.0, None, ALU.mult))

    s_x = sem("s_x")
    s_job = sem("s_job")
    s_job_done = sem("s_job_done")
    s_job_act = sem("s_job_act")
    s_xn = sem("s_xn")
    s_qk = sem("s_qk")
    s_scores = sem("s_scores")
    s_probs = sem("s_probs")
    s_pv = sem("s_pv")
    s_o = sem("s_o")
    s_pre = sem("s_pre")
    s_var = sem("s_var")
    s_rstd = sem("s_rstd")
    s_res = sem("s_res")
    s_sumsq = sem("s_sumsq")
    s_inv = sem("s_inv")
    s_post = sem("s_post")

    def wait_taken(eng, img, job):
        n = job if isinstance(job, int) else jobs_of(img).index(job)
        if n < 0:
            img, n = img - 1, n + len(jobs_of(img - 1))
        scalar = jobs_of(img)[n][0] in ON_SCALAR
        eng.wait_ge(s_job_act if scalar else s_job_done,
                    jobs_before(img, scalar) + count(jobs_of(img)[:n + 1], scalar))

    def sp_image(sp, img):
        if not isinstance(img, int) or img + 2 < B:
            sp.wait_ge(s_job, jobs_before(img) + jobs_of(img).index(("x", NT - 1)) + 1)
            nxt = img + 2 if isinstance(img, int) else (img + 2) % B
            sp.dma_start(x_in[:, :, :], x_img[nxt]).then_inc(s_x, 16)
        if has_post(img):
            wait_taken(sp, img, ("c", NT - 1))
            sp.dma_start(x1_img[img - 1], x1[:, :, :]).then_inc(s_x1_free, 16)

    def scores(pe, img, par, u):
        g, m, j = u // (UNITS // 2), u % (UNITS // 2) // GH, u % GH
        h = g * GH + j
        if u == 0:
            wait_taken(pe, img, -1)
        if not (isinstance(img, int) and UNITS * img + u < 2):
            pe.wait_ge(s_probs, UNITS * img + (u - 1))
        for f in range(2):
            mm = pe.matmul(ps_s[:, u % 2, f, :], stacks[:, par, 1, h, m * P:(m + 1) * P],
                           stacks[:, par, 0, h, f * HALF:(f + 1) * HALF], start=True, stop=True)
        mm.then_inc(s_scores, 1)

    def pv(pe, img, par, k):
        p, f = k // 2, k % 2
        g, m = p // (UNITS // 4), p % (UNITS // 4) // 2
        if f == 0:
            pe.wait_ge(s_probs, UNITS * img + 2 * p + 2)
        if p % (UNITS // 4) == 0 and not (isinstance(img, int) and img == 0 and g == 0):
            pe.wait_ge(s_o, 4 * img + 2 * g + f - 1)
        for u in (2 * p, 2 * p + 1):
            j = u % GH
            mm = pe.matmul(ps_o[32 * j:32 * j + 32, f, :], v_aug[:, par, m, g * GH + j, :],
                           probs[:, u % PRING, f * HALF:(f + 1) * HALF], start=(m == 0), stop=(m == NT - 1))
        mm.then_inc(s_pv, 1)

    def products(pe, out, slot, cols):
        for i, (c, w, rows) in enumerate(PRODUCTS):
            mm = pe.matmul(out, xn_t[0:rows, slot, c, :], w_qkv[0:rows, w, cols], start=(i == 0), stop=(i == 4))
        return mm

    def pe_job(pe, img, par, n, job):
        kind, t = job
        bank = ps_m[:, n % 2, :]
        if not (isinstance(img, int) and img == -1 and n < 2):
            wait_taken(pe, img, n - 2)
        tile = slice(t * P, (t + 1) * P)
        npre = NT * (img + 1)
        if kind == "x":
            if t == 0:
                pe.wait_ge(s_x, 16 * (img + 2))
            for k in range(2):
                mm = pe.transpose(bank[:, k * HC:(k + 1) * HC], x_in[:, k, tile], ident[0:HC, 0:HC])
        elif kind == "n":
            pe.wait_ge(s_xn, npre + t + 1)
            b16 = bank.bitcast(F16)
            for k in range(3):
                mm = pe.transpose(b16[:, k * P:(k + 1) * P], xn_split[:, t % 2, k * P:(k + 1) * P], ident16[:, :])
        elif kind in "uv":
            if kind == "u":
                wait_taken(pe, img, ("n", t))
            off = QCOLS * "uv".index(kind)
            mm = products(pe, bank[:, 0:QCOLS], t % 2, slice(off, off + QCOLS))
        elif kind in "qk":
            if kind == "q":
                pe.wait_ge(s_qk, npre + t + 1)
            b16 = bank.bitcast(F16)
            for h in range(NH):
                mm = pe.transpose(b16[0:4 * HD, h * P:(h + 1) * P],
                                  qk_split[:, t % QRING, NH * "qk".index(kind) + h, :, :].rearrange("p a d -> p (a d)"),
                                  ident16[:, :])
        elif kind == "a":
            if t == 0:
                pe.wait_ge(s_o, 4 * img)
            for g in range(2):
                mm = pe.transpose(bank[:, g * P:(g + 1) * P], o_sb[:, 1 - par, g, tile], ident[:, :])
        elif kind == "b":
            wait_taken(pe, img, ("a", t))
            for k in range(2):
                mm = pe.transpose(bank[0:HC, k * P:(k + 1) * P], o_norm[:, t % 2, k * HC:(k + 1) * HC], ident[:, :])
        else:
            wait_taken(pe, img, ("b", t))
            for k in range(2):
                mm = pe.matmul(bank[:, 0:C], o_t[:, t % 2, k, :], w_proj[:, k, :], start=(k == 0), stop=(k == 1))
        mm.then_inc(s_job, 1)

    def pe_image(pe, img, par, attend=True):
        n = 0
        for u in range(UNITS):
            if attend:
                scores(pe, img, par, u)
            if u >= 3 and attend:
                pv(pe, img, par, u - 3)
            elif u < 3 and has_post(img):
                pv(pe, img - 1, 1 - par, UNITS - 3 + u)
            for job in jobs_at(img, u):
                pe_job(pe, img, par, n, job)
                n += 1

    def act_image(act, img, par, attend=True):
        n = 0
        for u in range(UNITS):
            if attend:
                act.wait_ge(s_scores, UNITS * img + u + 1)
                if not (isinstance(img, int) and UNITS * img + u < PRING):
                    act.wait_ge(s_pv, UNITS * img + 2 * ((u - PRING) // 2) + 2)
                h = u // (UNITS // 2) * GH + u % GH
                act.activation(probs[:, u % PRING, :], ps_s[:, u % 2, :, :].rearrange("p f n -> p (f n)"),
                               ACT.Exp, bias=shift[:, 1, h:h + 1], scale=temps[:, h:h + 1]).then_inc(s_probs, 1)
            for kind, t in jobs_at(img, u):
                if kind in ON_SCALAR:
                    act.wait_ge(s_job, jobs_before(img) + n + 1)
                if kind == "n":
                    act.activation(xn_t[:, t % 2, :, :].rearrange("p k n -> p (k n)"),
                                   ps_m[:, n % 2, :].bitcast(F16)[:, 0:3 * P], ACT.Copy).then_inc(s_job_act, 1)
                elif kind in "qk":
                    act.activation(stacks[:, 1 - par, "qk".index(kind), :, t * P:(t + 1) * P],
                                   ps_m[:, n % 2, :].bitcast(F16)[0:KROWS, :].rearrange("p (h n) -> p h n", h=NH),
                                   ACT.Copy).then_inc(s_job_act, 1)
                n += 1

    def take_o(dve, img, par, g, f):
        dve.wait_ge(s_pv, UNITS * img + UNITS // 2 * (g + 1) - 1 + f)
        dve.tensor_copy(o_sb[:, par, g, f * HALF:(f + 1) * HALF], ps_o[:, f, :]).then_inc(s_o, 1)

    def dve_job(dve, img, par, n, job, pre, post):
        kind, t = job
        done = jobs_before(img, False) + count(jobs_of(img)[:n], False)
        bank = ps_m[:, n % 2, :]
        dve.wait_ge(s_job, jobs_before(img) + n + 1)
        if not (isinstance(img, int) and img == -1 and n == 0):
            dve.wait_ge(s_job_done, done)
        nxt = 1 - par
        if kind == "x":
            if t == 0 and not (isinstance(img, int) and img == -1):
                dve.wait_ge(s_res, img + 1)
            dve.bn_stats(stats[:, t, :], bank[:, 0:C])
            dve.tensor_copy(x_tok[:, t, :], bank[:, 0:C]).then_inc(s_job_done, 1)
        elif kind == "u":
            dve.scalar_tensor_tensor(qk[:, t, :, :].rearrange("p h d -> p (h d)")[:, 0:QCOLS], bank[:, 0:QCOLS],
                                     1.0 / WSCALE, bias_qkv[:, 0:QCOLS], ALU.mult, ALU.add).then_inc(s_job_done, 1)
        elif kind == "v":
            dve.scalar_tensor_tensor(v_aug[:, nxt, t, :, 0:HD], bank[:, HC:HC + C].rearrange("p (h d) -> p h d", d=HD),
                                     1.0 / WSCALE, bias_qkv[:, 2 * C:QKV].rearrange("p (h d) -> p h d", d=HD),
                                     ALU.mult, ALU.add)
            dve.scalar_tensor_tensor(qk[:, t, :, :].rearrange("p h d -> p (h d)")[:, QCOLS:2 * C], bank[:, 0:HC],
                                     1.0 / WSCALE, bias_qkv[:, QCOLS:2 * C], ALU.mult, ALU.add).then_inc(s_job_done, 1)
        elif kind == "a":
            o = bank[:, 0:2 * P].rearrange("p (h d) -> p h d", d=32)
            post.now(dve.reciprocal(o_rec[:, :], o[:, :, HD]))
            dve.tensor_tensor(o_norm[:, t % 2, :].rearrange("p (h d) -> p h d", d=HD), o[:, :, 0:HD],
                              o_rec[:, :].unsqueeze(2).to_broadcast([P, NH, HD]), ALU.mult).then_inc(s_job_done, 1)
        elif kind == "b":
            dve.tensor_copy(o_t[:, t % 2, :, :].rearrange("p k n -> p (k n)"),
                            bank[0:HC, 0:2 * P]).then_inc(s_job_done, 1)
        else:
            if t == 0:
                dve.wait_ge(s_x1_free, 16 * img)
                if not has_pre(img):
                    dve.wait_ge(s_res, img)
            dve.tensor_tensor(x1[:, t, :], bank[:, 0:C], x_res[:, nxt, t, :], ALU.add).then_inc(s_job_done, 1)

    def split_rows(dve, img, t, pre):
        if t == 0:
            dve.wait_ge(s_rstd, img + 2)
        else:
            dve.wait_ge(s_xn, NT * (img + 1) + t)
        if t >= 2:
            wait_taken(dve, img, ("n", t - 2))
        pre.now(dve.tensor_scalar(xn[:, :], x_tok[:, t, :], mean[:, t:t + 1], rstd[:, t:t + 1],
                                  ALU.subtract, ALU.mult))
        pre.now(dve.tensor_copy(xn_split[:, t % 2, 0:C], xn[:, :]))
        dve.tensor_tensor(xn_split[:, t % 2, C:2 * C], xn[:, :], xn_split[:, t % 2, 0:C],
                          ALU.subtract).then_inc(s_xn, 1)

    def head_norms(dve, img, t, pre):
        wait_taken(dve, img, ("v", t))
        if not (isinstance(img, int) and img == -1 and t == 0):
            dve.wait_ge(s_sumsq, NT * (img + 1) + t)
        pre.now(dve.tensor_tensor(qk_sq[:, :, :], qk[:, t, :, :], qk[:, t, :, :], ALU.mult))
        dve.tensor_reduce(sumsq[:, t, :], qk_sq[:, :, :], AX.X, ALU.add).then_inc(s_sumsq, 1)

    def split_heads(dve, img, t, pre, part):
        q2, k2 = (qk[:, t, NH * i:NH * (i + 1), :].unsqueeze(2).to_broadcast([P, NH, 2, HD]) for i in range(2))
        qs, ks = (qk_split[:, t % QRING, NH * i:NH * (i + 1), :, :] for i in range(2))
        if part == 0:
            dve.wait_ge(s_inv, NT * (img + 1) + t + 1)
            pre.now(dve.scalar_tensor_tensor(qk[:, t, :, :],
                                             inv_norm[:, t, :].unsqueeze(2).to_broadcast([P, 2 * NH, HD]),
                                             1.0 / NORM_EPS, qk[:, t, :, :], ALU.min, ALU.mult))
        elif part == 1:
            if t >= QRING:
                wait_taken(dve, img, ("k", t - QRING))
            pre.mark(dve.tensor_copy(qs[:, :, 0:4:2, :], q2))
            pre.now(dve.tensor_copy(ks[:, :, 0:2, :], k2))
            pre.mark(dve.tensor_tensor(qs[:, :, 1:4:2, :], q2, qs[:, :, 0:4:2, :], ALU.subtract))
        else:
            dve.tensor_tensor(ks[:, :, 2:4, :], k2, ks[:, :, 0:2, :], ALU.subtract).then_inc(s_qk, 1)

    def pool_image(pool, img, par):
        pool.wait_ge(s_var, img + 2)
        pool.tensor_tensor(rstd[:, :], var[:, :], minus_half[:, 0:NT], ALU.pow).then_inc(s_rstd, 1)
        for t in range(NT):
            pool.wait_ge(s_sumsq, NT * (img + 1) + t + 1)
            pool.tensor_tensor(inv_norm[:, t, :], sumsq[:, t, :], minus_half[:, :], ALU.pow).then_inc(s_inv, 1)
        if has_post(img):
            wait_taken(pool, img, ("c", NT - 1))
        else:
            wait_taken(pool, img, ("x", NT - 1))
        pool.tensor_tensor(x_res[:, 1 - par, :, :], x_tok[:, :, :],
                           bias_proj[:, :].unsqueeze(1).to_broadcast([P, NT, C]), ALU.add).then_inc(s_res, 1)

    def dve_image(dve, img, par, attend=True):
        n = 0
        pre = Steps(dve, s_pre, PRE_STEPS * (img + 1))
        post = Steps(dve, s_post, POST_STEPS * (img - 1))
        if has_pre(img) and not (isinstance(img, int) and img == -1):
            dve.wait_ge(s_xn, NT * (img + 1))
            dve.wait_ge(s_qk, NT * (img + 1))
        for u in range(UNITS):
            if u in (1, 2) and has_post(img):
                take_o(dve, img - 1, 1 - par, 1, u - 1)
            if u in (33, 34) and attend:
                take_o(dve, img, par, 0, u - 33)
            for job in jobs_at(img, u):
                if job[0] not in ON_SCALAR:
                    dve_job(dve, img, par, n, job, pre, post)
                n += 1
            if has_pre(img):
                if u == NT:
                    wait_taken(dve, img, ("x", NT - 1))
                    mean_and_var(dve, pre, stats, mean[:, :], var[:, :], tmp8[:, :], LN1_EPS, s_var)
                if u == ROUND0 - 2:
                    for t in range(2):
                        split_rows(dve, img, t, pre)
                r, v = divmod(u - ROUND0, ROUND)
                if v == 1 and 0 <= r < NT:
                    head_norms(dve, img, r, pre)
                if v == 2 and 0 <= r and r + 2 < NT:
                    split_rows(dve, img, r + 2, pre)
                if v in (0, 3, 4) and 0 < r <= NT:
                    split_heads(dve, img, r - 1, pre, (0, 3, 4).index(v))
        if has_post(img):
            assert post.n == POST_STEPS, post.n
        if has_pre(img):
            assert pre.n == PRE_STEPS, (pre.n, PRE_STEPS)

    with nc.Block() as block:
        @block.sync
        def _(sp):
            sp.dma_start(x_in[:, :, :], x_img[0]).then_inc(s_x, 16)
            sp_image(sp, -1)
            sp_image(sp, 0)
            with sp.Fori(0, B // 2 - 1) as i:
                for k in range(2):
                    sp_image(sp, i * 2 + 1 + k)
            sp_image(sp, B - 1)
            sp_image(sp, B)
            sp.wait_ge(s_x1_free, 16 * (B + 1))

        @block.tensor
        def _(pe):
            pe_image(pe, -1, 1, attend=False)
            pe_image(pe, 0, 0)
            with pe.Fori(0, B // 2 - 1) as i:
                for k in range(2):
                    pe_image(pe, i * 2 + 1 + k, 1 - k)
            pe_image(pe, B - 1, 1)
            pe_image(pe, B, 0, attend=False)

        @block.scalar
        def _(act):
            act_image(act, -1, 1, attend=False)
            act_image(act, 0, 0)
            with act.Fori(0, B // 2 - 1) as i:
                for k in range(2):
                    act_image(act, i * 2 + 1 + k, 1 - k)
            act_image(act, B - 1, 1)

        @block.gpsimd
        def _(pool):
            pool_image(pool, -1, 1)
            pool_image(pool, 0, 0)
            with pool.Fori(0, B // 2 - 1) as i:
                for k in range(2):
                    pool_image(pool, i * 2 + 1 + k, 1 - k)

        @block.vector
        def _(dve):
            dve_image(dve, -1, 1, attend=False)
            dve_image(dve, 0, 0)
            with dve.Fori(0, B // 2 - 1) as i:
                for k in range(2):
                    dve_image(dve, i * 2 + 1 + k, 1 - k)
            dve_image(dve, B - 1, 1)
            dve_image(dve, B, 0, attend=False)


BT = 4
BTOK = BT * P
NBLK = B * NTOK // BTOK
STEPS = NE * NK
LAG = 2
HBUF, HSPLIT = 3, 4
MLP_PRE_STEPS = 59
SPLIT_STEPS = 3
F_AT, N_AT, G_AT = 4, 11, 15
EXP_AT, GATE_AT = 16, 17


def mlp_jobs_at(blk, n):
    post = not isinstance(blk, int) or blk >= 1
    pre = not isinstance(blk, int) or blk + 1 < NBLK
    jobs = []
    if post and F_AT <= n < F_AT + BT:
        jobs.append(("f", n - F_AT))
    if pre and N_AT <= n < N_AT + BT:
        jobs.append(("n", n - N_AT))
    if pre and n == G_AT:
        jobs.append(("g", 0))
    return jobs


def mlp_job_base(blk):
    if isinstance(blk, int) and blk <= 0:
        return (BT + 1) * (blk + 1)
    if isinstance(blk, int) and blk == NBLK:
        return mlp_job_base(blk - 1) + BT
    return 2 * (BT + 1) + (2 * BT + 1) * (blk - 1)


def mlp_phase(nc, ctx, x1_tokens, gate_w, gate_b, w1, b1, w2, b2, out):
    def sb(name, shape, dt=F32):
        return ctx.enter_context(nc.sbuf_tensor(name, shape, dt))

    def sem(name):
        return ctx.enter_context(nc.semaphore(name))

    x1_blk = x1_tokens.rearrange("(q t p) c -> q p t c", p=P, t=BT)
    out_img = out.rearrange("b (k c) h w -> b c k (h w)", k=2)

    ident = sb("m_ident", [P, P])
    ident16 = sb("m_ident16", [P, P], F16)
    w1_sb = sb("w1_sb", [P, NE, 5, HID], F16)
    w2_sb = sb("w2_sb", [P, NE, 2, NK, C], F16)
    wg_sb = sb("wg_sb", [P, 5, NE], F16)
    bias1 = sb("bias1", [P, NE * NK])
    bias2 = sb("bias2", [P, NE, C])
    bias_g = sb("bias_g", [P, NE])
    lower = sb("lower", [P, NE, NE])
    stage1 = sb("stage1", [P, 2, 3, HID])
    stage2 = sb("stage2", [P, 2, NK, C])
    stage_g = sb("stage_g", [P, 3, NE])
    stage_b = sb("stage_b", [NE * NK, P])
    x1_in = sb("x1_in", [P, BT, C])
    stats = sb("m_stats", [P, BT, 6])
    mean = sb("m_mean", [P, BT])
    var = sb("m_var", [P, BT])
    rstd = sb("m_rstd", [P, BT])
    tmp4 = sb("m_tmp4", [P, BT])
    xn = sb("m_xn", [P, BT, C])
    xn_split = sb("m_xn_split", [P, BT, 2 * C], F16)
    xn_t = sb("m_xn_t", [P, 2, 3, BTOK], F16)
    h_f32 = sb("h_f32", [P, HBUF, BTOK])
    h_split = sb("h_split", [P, HSPLIT, 2, BTOK], F16)
    acc = sb("acc", [P, 2, BT, C])
    logits = sb("logits", [P, BT, NE])
    top = sb("top", [P, BT])
    expo = sb("expo", [P, BT, NE])
    prob = sb("prob", [P, BT, NE])
    beats = sb("beats", [P, BT, NE, NE])
    ties = sb("ties", [P, BT, NE, NE])
    rank = sb("rank", [P, BT, NE])
    total = sb("total", [P, BT])
    gates = sb("gates", [P, 2, BT, NE])
    gates_w = sb("gates_w", [P, 2, BT, NE])
    y_out = sb("y_out", [HC, 2, BTOK])

    ps_h = ctx.enter_context(nc.psum_tensor("ps_h", [P, HBUF, BTOK], F32))
    ps_y = ctx.enter_context(nc.psum_tensor("ps_y", [P, 2, 2, 512], F32))
    ps_j = ctx.enter_context(nc.psum_tensor("ps_j", [P, 512], F32))

    s_zero, s_const = sem("m_zero"), sem("m_const")
    s_wl = [sem(f"m_w1_load{e}") for e in range(2)]
    s_bl = sem("m_b_load")
    s_b1 = sem("m_b1")
    s_hi = sem("m_hi")
    s_setup = sem("m_setup")
    s_out = sem("m_out")

    def weight_parts(e):
        a, b = stage1[:, e % 2, :, :], stage2[:, e % 2, :, :]
        return [(a[:, 0, :], w1_sb[:, e, 0, :], w1_sb[:, e, 3, :]),
                (a[0:64, 1, :], w1_sb[0:64, e, 1, :], w1_sb[0:64, e, 4, :]),
                (b, w2_sb[:, e, 0, :, :], w2_sb[:, e, 1, :, :])]

    gate_parts = [(stage_g[:, 0, :], wg_sb[:, 0, :], wg_sb[:, 3, :]),
                  (stage_g[0:64, 1, :], wg_sb[0:64, 1, :], wg_sb[0:64, 4, :])]

    with nc.Block() as block:
        @block.sync
        def _(sp):
            for e in range(NE):
                if e >= 2:
                    sp.wait_ge(s_setup, SPLIT_STEPS * (e - 1))
                for s, (lo, hi, at) in enumerate(((0, P, 0), (P, C, 0), (64, C, 0))):
                    sp.dma_start(stage1[at:at + hi - lo, e % 2, s, :], w1[e, lo:hi, :]).then_inc(s_wl[e % 2], 16)
                sp.dma_start(stage1[64:P, e % 2, 1, :], w1[e, 0:64, :]).then_inc(s_wl[e % 2], 16)
                sp.dma_start(stage2[:, e % 2, :, :], w2[e].rearrange("(k p) c -> p k c", p=P)).then_inc(s_wl[e % 2], 16)

        @block.scalar
        def _(act):
            for s, (lo, hi) in enumerate(((0, P), (P, C), (64, C))):
                act.dma_start(stage_g[0:hi - lo, s, :], gate_w[lo:hi, :]).then_inc(s_bl, 16)
            act.dma_start(stage_g[64:P, 1, :], gate_w[0:64, :]).then_inc(s_bl, 16)
            act.dma_start(stage_b[:, :], b1.rearrange("e (k p) -> (e k) p", p=P)).then_inc(s_bl, 16)
            act.dma_start(bias2[:, :, :], b2.rearrange("(a e) c -> a e c", a=1).to_broadcast([P, NE, C])).then_inc(s_bl, 16)
            act.dma_start(bias_g[:, :], gate_b.rearrange("(a e) -> a e", a=1).to_broadcast([P, NE])).then_inc(s_bl, 16)
            for e in range(NE):
                act.wait_ge(s_wl[e % 2], 80 * (e // 2 + 1))
                act.activation(w1_sb[:, e, 0:3, :], stage1[:, e % 2, :, :], ACT.Copy, scale=WSCALE)
                act.activation(w2_sb[:, e, 0, :, :], stage2[:, e % 2, :, :], ACT.Copy, scale=WSCALE).then_inc(s_hi, 1)
            act.wait_ge(s_bl, 16 * 7)
            act.activation(wg_sb[:, 0:3, :], stage_g[:, :, :], ACT.Copy, scale=WSCALE).then_inc(s_hi, 1)

        @block.gpsimd
        def _(pool):
            pool.memset(ident[:, :], 0.0).then_inc(s_zero, 1)
            pool.memset(ident16[:, :], 0.0).then_inc(s_zero, 1)
            pool.memset(lower[:, :, :], 0.0).then_inc(s_zero, 1)
            pool.wait_ge(s_zero, 3)
            for m in (ident, ident16):
                pool.affine_select(out=m[:, :], in_=m[:, :], compare_op=ALU.not_equal, fill=1.0, base=0,
                                   pattern=[[-1, P]], channel_multiplier=1).then_inc(s_const, 1)
            own = Steps(pool, s_const, 2)
            for i in range(1, NE):
                own.now(pool.memset(lower[:, i, 0:i], 1.0))
            pool.memset(y_out[:, 0, 0:1], 0.0).then_inc(s_out, 16)

        @block.tensor
        def _(pe):
            pe.wait_ge(s_const, 1)
            pe.wait_ge(s_bl, 16 * 7)
            pe.transpose(ps_j[:, 0:NE * NK], stage_b[:, :], ident[0:NE * NK, 0:NE * NK]).then_inc(s_b1, 1)

        @block.vector
        def _(dve):
            st = Steps(dve, s_setup)

            for e in range(NE):
                dve.wait_ge(s_hi, e + 1)
                for a, hi, lo in weight_parts(e):
                    st.mark(dve.scalar_tensor_tensor(lo, a, WSCALE, hi, ALU.mult, ALU.subtract))
            dve.wait_ge(s_hi, NE + 1)
            for a, hi, lo in gate_parts:
                st.mark(dve.scalar_tensor_tensor(lo, a, WSCALE, hi, ALU.mult, ALU.subtract))
            dve.wait_ge(s_b1, 1)
            dve.tensor_copy(bias1[:, :], ps_j[:, 0:NE * NK])

    s_x1 = sem("m_x1")
    s_job = sem("m_job")
    s_job_done = sem("m_job_done")
    s_xn = sem("m_xn")
    s_w1 = sem("m_h")
    s_gelu = sem("m_gelu")
    s_h = sem("m_hsplit")
    s_w2 = sem("m_y")
    s_acc = sem("m_acc")
    s_logit = sem("m_logit")
    s_exp = sem("m_exp")
    s_acc0 = sem("m_acc0")
    s_pre = sem("m_pre")
    s_own = sem("m_own")

    def first(blk):
        return isinstance(blk, int) and blk == -1

    def sp_block(sp, blk, img, half):
        if not isinstance(blk, int) or blk >= 1:
            sp.wait_ge(s_job_done, mlp_job_base(blk) + BT)
            sp.dma_start(out_img[img][:, :, half * BTOK:(half + 1) * BTOK], y_out[:, :, :]).then_inc(s_out, 16)
        if not isinstance(blk, int) or blk + 2 < NBLK:
            nxt = blk + 2 if isinstance(blk, int) else (blk + 2) % NBLK
            sp.wait_ge(s_acc0, blk + 2)
            sp.dma_start(x1_in[:, :, :], x1_blk[nxt]).then_inc(s_x1, 16)

    def first_product(pe, blk, par, n):
        e, k = n // NK, n % NK
        if n == 0:
            pe.wait_ge(s_job_done, mlp_job_base(blk))
        if not (isinstance(blk, int) and STEPS * blk + n < HBUF):
            pe.wait_ge(s_gelu, STEPS * blk + n - HBUF + 1)
        for i, (c, w, rows) in enumerate(PRODUCTS):
            mm = pe.matmul(ps_h[:, n % HBUF, :], w1_sb[0:rows, e, w, k * P:(k + 1) * P], xn_t[0:rows, par, c, :],
                           start=(i == 0), stop=(i == 4))
        mm.then_inc(s_w1, 1)

    def second_product(pe, blk, n):
        e, k = n // NK, n % NK
        pe.wait_ge(s_h, STEPS * blk + n + 1)
        if k == 0 and not (isinstance(blk, int) and NE * blk + e < 2):
            pe.wait_ge(s_acc, NE * blk + e - 1)
        for t in range(BT):
            y = ps_y[:, e % 2, t // 2, (t % 2) * C:(t % 2 + 1) * C]
            tok = slice(t * P, (t + 1) * P)
            for i, (hp, wp) in enumerate(((0, 0), (0, 1), (1, 0))):
                mm = pe.matmul(y, h_split[:, n % HSPLIT, hp, tok], w2_sb[:, e, wp, k, :],
                               start=(k == 0 and i == 0 and t % 2 == 0), stop=(k == NK - 1 and i == 2),
                               skip_group_check=True)
        mm.then_inc(s_w2, 1)

    def pe_mlp_job(pe, blk, par, base, j, job):
        kind, t = job
        if not (first(blk) and j == 0):
            pe.wait_ge(s_job_done, base + j)
        if kind == "f":
            if t == 0:
                pe.wait_ge(s_acc, NE * blk)
            for k in range(2):
                mm = pe.transpose(ps_j[0:HC, k * P:(k + 1) * P], acc[:, 1 - par, t, k * HC:(k + 1) * HC], ident[:, :])
        elif kind == "n":
            if t == 0:
                pe.wait_ge(s_xn, blk + 2)
            b16 = ps_j[:, :].bitcast(F16)
            for k in range(3):
                mm = pe.transpose(b16[:, k * P:(k + 1) * P], xn_split[:, t, k * P:(k + 1) * P], ident16[:, :])
        else:
            for t in range(BT):
                for i, (c, w, rows) in enumerate(PRODUCTS):
                    mm = pe.matmul(ps_j[:, t * NE:(t + 1) * NE], xn_t[0:rows, 1 - par, c, t * P:(t + 1) * P],
                                   wg_sb[0:rows, w, :], start=(i == 0), stop=(i == 4))
        mm.then_inc(s_job, 1)

    def pe_block(pe, blk, par, main=True):
        base, j = mlp_job_base(blk), 0
        for n in range(STEPS):
            if main:
                first_product(pe, blk, par, n)
            if n >= LAG and main:
                second_product(pe, blk, n - LAG)
            elif n < LAG and (not isinstance(blk, int) or blk >= 1):
                second_product(pe, blk - 1, STEPS - LAG + n)
            for job in mlp_jobs_at(blk, n):
                pe_mlp_job(pe, blk, par, base, j, job)
                j += 1

    def act_block(act, blk, main=True):
        for n in range(STEPS):
            if main:
                act.wait_ge(s_w1, STEPS * blk + n + 1)
                if not (isinstance(blk, int) and STEPS * blk + n < HSPLIT):
                    act.wait_ge(s_w2, STEPS * blk + n - HSPLIT + 1)
                act.activation(h_split[:, n % HSPLIT, 0, :], ps_h[:, n % HBUF, :], ACT.Gelu, bias=bias1[:, n:n + 1],
                               scale=1.0 / WSCALE)
                if not (isinstance(blk, int) and STEPS * blk + n < HBUF):
                    act.wait_ge(s_h, STEPS * blk + n - HBUF + 1)
                act.activation(h_f32[:, n % HBUF, :], ps_h[:, n % HBUF, :], ACT.Gelu, bias=bias1[:, n:n + 1],
                               scale=1.0 / WSCALE).then_inc(s_gelu, 1)
            if n == EXP_AT and (not isinstance(blk, int) or blk + 1 < NBLK):
                act.wait_ge(s_logit, blk + 2)
                act.activation(expo[:, :, :], logits[:, :, :], ACT.Exp).then_inc(s_exp, 1)

    def pool_block(pool, blk):
        for n in range(STEPS):
            pool.wait_ge(s_gelu, STEPS * blk + n + 1)
            if not (isinstance(blk, int) and STEPS * blk + n < HSPLIT):
                pool.wait_ge(s_w2, STEPS * blk + n - HSPLIT + 1)
            pool.tensor_tensor(h_split[:, n % HSPLIT, 1, :], h_f32[:, n % HBUF, :], h_split[:, n % HSPLIT, 0, :],
                               ALU.subtract).then_inc(s_h, 1)

    def add_expert(dve, blk, par, e, own):
        dve.wait_ge(s_w2, STEPS * blk + (e + 1) * NK)
        for t in range(BT):
            ins = dve.scalar_tensor_tensor(acc[:, par, t, :], ps_y[:, e % 2, t // 2, (t % 2) * C:(t % 2 + 1) * C],
                                           gates_w[:, par, t, e:e + 1], acc[:, par, t, :], ALU.mult, ALU.add)
            if t < BT - 1:
                own.mark(ins)
        ins.then_inc(s_acc, 1)
        dve.wait_ge(s_acc, NE * blk + e + 1)

    def mlp_dve_job(dve, blk, par, base, j, job, pre):
        kind, t = job
        dve.wait_ge(s_job, base + j + 1)
        if not (first(blk) and j == 0):
            dve.wait_ge(s_job_done, base + j)
        if kind == "f":
            if t == 0:
                dve.wait_ge(s_out, 16 * blk)
            dve.tensor_copy(y_out[:, :, t * P:(t + 1) * P],
                            ps_j[0:HC, 0:2 * P].rearrange("p (k n) -> p k n", k=2)).then_inc(s_job_done, 1)
        elif kind == "n":
            dve.tensor_copy(xn_t[:, 1 - par, :, t * P:(t + 1) * P],
                            ps_j[:, :].bitcast(F16)[:, 0:3 * P].rearrange("p (k n) -> p k n", k=3)).then_inc(s_job_done, 1)
        else:
            dve.scalar_tensor_tensor(logits[:, :, :], ps_j[:, 0:BT * NE].rearrange("p (t e) -> p t e", e=NE),
                                     1.0 / WSCALE, bias_g[:, :].unsqueeze(1).to_broadcast([P, BT, NE]),
                                     ALU.mult, ALU.add).then_inc(s_job_done, 1)
            dve.wait_ge(s_job_done, base + j + 1)
            pre.now(dve.tensor_reduce(top[:, :], logits[:, :, :], AX.X, ALU.max))
            dve.tensor_tensor(logits[:, :, :], logits[:, :, :], top[:, :].unsqueeze(2).to_broadcast([P, BT, NE]),
                              ALU.subtract).then_inc(s_logit, 1)

    def gate_weights(dve, blk, nxt, pre):
        dve.wait_ge(s_exp, blk + 2)
        dve.wait_ge(s_logit, blk + 2)
        bc = lambda v: v.unsqueeze(2).to_broadcast([P, BT, NE])
        pre.now(dve.tensor_reduce(total[:, :], expo[:, :, :], AX.X, ALU.add))
        pre.now(dve.reciprocal(total[:, :], total[:, :]))
        pre.now(dve.tensor_tensor(prob[:, :, :], expo[:, :, :], bc(total[:, :]), ALU.mult))
        p_i = prob[:, :, :].unsqueeze(3).to_broadcast([P, BT, NE, NE])
        p_j = prob[:, :, :].unsqueeze(2).to_broadcast([P, BT, NE, NE])
        pre.mark(dve.tensor_tensor(beats[:, :, :, :], p_j, p_i, ALU.is_gt))
        pre.now(dve.tensor_tensor(ties[:, :, :, :], p_j, p_i, ALU.is_equal))
        pre.now(dve.tensor_tensor(ties[:, :, :, :], ties[:, :, :, :],
                                  lower[:, :, :].unsqueeze(1).to_broadcast([P, BT, NE, NE]), ALU.mult))
        pre.now(dve.tensor_tensor(beats[:, :, :, :], beats[:, :, :, :], ties[:, :, :, :], ALU.add))
        pre.now(dve.tensor_reduce(rank[:, :, :], beats[:, :, :, :], AX.X, ALU.add))
        pre.now(dve.tensor_scalar(rank[:, :, :], rank[:, :, :], 2.0, None, ALU.is_lt))
        pre.now(dve.tensor_tensor(prob[:, :, :], prob[:, :, :], rank[:, :, :], ALU.mult))
        pre.now(dve.tensor_reduce(total[:, :], prob[:, :, :], AX.X, ALU.add))
        pre.now(dve.tensor_scalar(total[:, :], total[:, :], 1e-9, None, ALU.add))
        pre.now(dve.reciprocal(total[:, :], total[:, :]))
        pre.now(dve.tensor_tensor(gates[:, nxt, :, :], prob[:, :, :], bc(total[:, :]), ALU.mult))
        pre.now(dve.tensor_scalar(gates_w[:, nxt, :, :], gates[:, nxt, :, :], 1.0 / WSCALE, None, ALU.mult))

    def start_acc(dve, blk, nxt, t, pre):
        src = x1_in[:, t, :]
        for e in range(NE):
            ins = dve.scalar_tensor_tensor(acc[:, nxt, t, :], bias2[:, e, :], gates[:, nxt, t, e:e + 1], src,
                                           ALU.mult, ALU.add)
            src = acc[:, nxt, t, :]
            if t < BT - 1 or e < NE - 1:
                pre.now(ins)
        if t == BT - 1:
            ins.then_inc(s_acc0, 1)
            dve.wait_ge(s_acc0, blk + 2)

    def dve_block(dve, blk, par, main=True):
        base, j = mlp_job_base(blk), 0
        has_pre = not isinstance(blk, int) or blk + 1 < NBLK
        has_post = not isinstance(blk, int) or blk >= 1
        nxt = 1 - par
        pre = Steps(dve, s_pre, MLP_PRE_STEPS * (blk + 1))
        own = Steps(dve, s_own, NE * (BT - 1) * blk)
        if has_post:
            own.base = own.base - (BT - 1)
        for n in range(STEPS):
            if n == 2 and has_post:
                add_expert(dve, blk - 1, nxt, NE - 1, own)
            if main and n in (8, 14, 20):
                add_expert(dve, blk, par, (n - 8) // NK, own)
            if has_pre:
                if n == 3:
                    dve.wait_ge(s_x1, 16 * (blk + 2))
                    for t in range(BT):
                        pre.mark(dve.bn_stats(stats[:, t, :], x1_in[:, t, :]))
                    pre.wait(pre.n)
                if n == 4:
                    mean_and_var(dve, pre, stats, mean[:, :], var[:, :], tmp4[:, :], LN2_EPS)
                if n in (5, 6, 7):
                    rsqrt(dve, pre, var[:, :], rstd[:, :], tmp4[:, :], n - 5)
                if n == 8:
                    if not first(blk):
                        dve.wait_ge(s_xn, blk + 1)
                    for t in range(BT):
                        pre.mark(dve.tensor_scalar(xn[:, t, :], x1_in[:, t, :], mean[:, t:t + 1],
                                                   rstd[:, t:t + 1], ALU.subtract, ALU.mult))
                    pre.wait(pre.n)
                if n == 9:
                    pre.now(dve.tensor_copy(xn_split[:, :, 0:C], xn[:, :, :]))
                if n == 10:
                    dve.tensor_tensor(xn_split[:, :, C:2 * C], xn[:, :, :], xn_split[:, :, 0:C],
                                      ALU.subtract).then_inc(s_xn, 1)
            for job in mlp_jobs_at(blk, n):
                mlp_dve_job(dve, blk, par, base, j, job, pre)
                j += 1
            if has_pre:
                if n == GATE_AT:
                    gate_weights(dve, blk, nxt, pre)
                if n in (18, 19, 21, 22):
                    start_acc(dve, blk, nxt, (18, 19, 21, 22).index(n), pre)
        if has_pre:
            assert pre.n == MLP_PRE_STEPS, pre.n

    with nc.Block() as block:
        @block.sync
        def _(sp):
            sp.dma_start(x1_in[:, :, :], x1_blk[0]).then_inc(s_x1, 16)
            sp_block(sp, -1, 0, 0)
            sp_block(sp, 0, 0, 0)
            with sp.Fori(0, NBLK // 2 - 1) as i:
                for k in range(2):
                    sp_block(sp, i * 2 + 1 + k, i, k)
            sp_block(sp, NBLK - 1, B - 1, 0)
            sp_block(sp, NBLK, B - 1, 1)
            sp.wait_ge(s_out, 16 * (NBLK + 1))

        @block.tensor
        def _(pe):
            pe_block(pe, -1, 1, main=False)
            pe_block(pe, 0, 0)
            with pe.Fori(0, NBLK // 2 - 1) as i:
                for k in range(2):
                    pe_block(pe, i * 2 + 1 + k, 1 - k)
            pe_block(pe, NBLK - 1, 1)
            pe_block(pe, NBLK, 0, main=False)

        @block.scalar
        def _(act):
            act_block(act, -1, main=False)
            act_block(act, 0)
            with act.Fori(0, NBLK // 2 - 1) as i:
                for k in range(2):
                    act_block(act, i * 2 + 1 + k)
            act_block(act, NBLK - 1)

        @block.gpsimd
        def _(pool):
            pool_block(pool, 0)
            with pool.Fori(0, NBLK // 2 - 1) as i:
                for k in range(2):
                    pool_block(pool, i * 2 + 1 + k)
            pool_block(pool, NBLK - 1)

        @block.vector
        def _(dve):
            dve_block(dve, -1, 1, main=False)
            dve_block(dve, 0, 0)
            with dve.Fori(0, NBLK // 2 - 1) as i:
                for k in range(2):
                    dve_block(dve, i * 2 + 1 + k, 1 - k)
            dve_block(dve, NBLK - 1, 1)
            dve_block(dve, NBLK, 0, main=False)


_INS = ['x', 'L0_conv_temperature', 'L0_conv_qkv_w', 'L0_conv_qkv_b', 'L0_conv_proj_w', 'L0_conv_proj_b',
        'L0_ffn_gate_w', 'L0_ffn_gate_b', 'L0_ffn_w1', 'L0_ffn_b1', 'L0_ffn_w2', 'L0_ffn_b2']
_OUTS = [((B, C, 32, 32), 'float32')]


def metaformer_block(nc, x, temp, qkv_w, qkv_b, proj_w, proj_b, gate_w, gate_b, w1, b1, w2, b2, out, x1_tokens=None):
    if x1_tokens is None:
        x1_tokens = nc.dram_tensor("x1_tokens", [B * NTOK, C], F32, kind="Internal").ap()
    with ExitStack() as ctx:
        attention_phase(nc, ctx, x, temp, qkv_w, qkv_b, proj_w, proj_b, x1_tokens)
    with ExitStack() as ctx:
        mlp_phase(nc, ctx, x1_tokens, gate_w, gate_b, w1, b1, w2, b2, out)


def kernel(**inputs):
    import numpy as _np
    import concourse.bacc as _bacc
    from concourse.bass_utils import run_bass_kernel_spmd as _run

    nc = _bacc.Bacc("TRN2", target_bir_lowering=False, num_devices=1)
    arrays, args = {}, []
    for name in _INS:
        a = _np.ascontiguousarray(inputs[name])
        arrays[f"in_{name}_dram"] = a
        args.append(nc.dram_tensor(f"in_{name}_dram", a.shape, mybir.dt.from_np(a.dtype), kind="ExternalInput").ap())
    for i, (shape, dtype) in enumerate(_OUTS):
        dt = mybir.dt.from_np(_np.dtype(dtype))
        args.append(nc.dram_tensor(f"out_{i}_dram", shape, dt, kind="ExternalOutput").ap())
    metaformer_block(nc, *args)
    r = _run(nc, [arrays], core_ids=[0])
    return r.results[0]["out_0_dram"]
```

```python
from contextlib import ExitStack

import concourse.bass as bass
from concourse import mybir

F32 = mybir.dt.float32
F16 = mybir.dt.float16
I32 = mybir.dt.int32
ALU = mybir.AluOpType
ACT = mybir.ActivationFunctionType
AX = mybir.AxisListType

B, C, NTOK = 16, 192, 1024
NH, HD = 8, 24
P = 128
HC = C // 2
NT = NTOK // P
HALF = 512
QKV = 3 * C
QCOLS = QKV // 2
WCOLS = QKV + C
WJ = WCOLS // HC
WSCALE = 64.0
OSCALE = 16.0
NE, HID = 4, 4 * C
NK = HID // P
WPIECES = 5
WUNIT = 12
EXP_RANGE = 60.0
KROWS = 4 * HD
GH = NH // 2
UNITS = NH * NT
PRING = 8
QRING = 2
LN1_EPS, LN2_EPS, NORM_EPS = 1e-6, 1e-5, 1e-12
MAGIC = 1597463007.0

PRODUCTS = [(0, 0, P), (1, 1, P), (2, 2, P), (0, 3, P), (1, 4, 64)]


class Steps:

    def __init__(self, eng, sem, base=0):
        self.eng, self.sem, self.base, self.n = eng, sem, base, 0

    def mark(self, ins):
        ins.then_inc(self.sem, 1)
        self.n += 1
        return self.n

    def wait(self, n):
        self.eng.wait_ge(self.sem, self.base + n)

    def now(self, ins):
        self.wait(self.mark(ins))


def rsqrt(eng, steps, v, y, t, part):
    if part == 0:
        rsqrt_guess(eng, steps, v, y, t)
    steps.now(eng.scalar_tensor_tensor(t, y, -0.5, y, ALU.mult, ALU.mult))
    steps.now(eng.tensor_tensor(t, t, v, ALU.mult))
    steps.now(eng.scalar_tensor_tensor(y, t, 1.5, y, ALU.add, ALU.mult))


def rsqrt_guess(eng, steps, v, y, t):
    steps.now(eng.tensor_scalar(t.bitcast(I32), v.bitcast(I32), 1, None, ALU.logical_shift_right))
    steps.now(eng.tensor_scalar(y.bitcast(I32), t.bitcast(I32), -1.0, MAGIC, ALU.mult, ALU.add))


def mean_and_var(eng, steps, stats, mean, var, t, eps, done=None):
    steps.mark(eng.tensor_tensor(mean, stats[:, :, 1], stats[:, :, 4], ALU.add))
    steps.mark(eng.tensor_tensor(t, stats[:, :, 1], stats[:, :, 4], ALU.subtract))
    steps.now(eng.tensor_tensor(var, stats[:, :, 2], stats[:, :, 5], ALU.add))
    steps.mark(eng.tensor_scalar(mean, mean, 0.5, 0.0, ALU.mult, ALU.add))
    steps.mark(eng.tensor_scalar(t, t, 0.5, 0.0, ALU.mult, ALU.add))
    steps.now(eng.tensor_scalar(var, var, 1.0 / C, eps, ALU.mult, ALU.add))
    steps.now(eng.tensor_tensor(t, t, t, ALU.mult))
    last = eng.tensor_tensor(var, var, t, ALU.add)
    if done is None:
        steps.now(last)
    else:
        last.then_inc(done, 1)


class Mlp:

    def __init__(self, nc, ctx):
        def sb(name, shape, dt=F32):
            return ctx.enter_context(nc.sbuf_tensor(name, shape, dt))

        even = sb("even", [P, 2 * NH * NTOK], F16)
        self.w1 = even[:, 0:NE * 5 * HID].rearrange("p (e s n) -> p e s n", e=NE, s=5)
        self.stacks_even = even[0:KROWS, :].rearrange("p (a h n) -> p a h n", a=2, h=NH)
        heads = sb("heads", [P, NE * 2 * NK * C], F16)
        nqk = NT * 2 * C
        self.w2 = heads[:, :].rearrange("p (e s k c) -> p e s k c", e=NE, s=2, k=NK)
        self.qk = heads[:, 0:2 * nqk].bitcast(F32).rearrange("p (t h d) -> p t h d", t=NT, h=2 * NH)
        self.qk_split = heads[:, 2 * nqk:2 * nqk + QRING * 8 * C].rearrange("p (r h a d) -> p r h a d", r=QRING, a=4, d=HD)
        tokens = sb("tokens", [P, 2 * NTOK + NT * C])
        self.stage1 = tokens[:, 0:3 * HID].rearrange("p (s n) -> p s n", s=3)
        self.stage2 = tokens[:, 3 * HID:3 * HID + NK * C].rearrange("p (k c) -> p k c", k=NK)
        self.x_in = tokens[0:HC, 0:2 * NTOK].rearrange("p (k n) -> p k n", k=2)
        self.x_tok = tokens[:, 2 * NTOK:].rearrange("p (t c) -> p t c", t=NT)
        self.stage_g = sb("stage_g", [P, 3, NE])
        self.stage_b = sb("stage_b", [NE * NK, P])
        self.bias2 = sb("bias2", [P, NE, C])
        self.bias_g = sb("bias_g", [P, NE])
        self.s_bl = ctx.enter_context(nc.semaphore("m_b_load"))
        self.s_load = ctx.enter_context(nc.semaphore("m_w_load"))
        self.s_split = ctx.enter_context(nc.semaphore("m_w_split"))

    def load_small(self, dma, gate_w, gate_b, b1, b2):
        for s, (lo, hi) in enumerate(((0, P), (P, C), (64, C))):
            dma(self.stage_g[0:hi - lo, s, :], gate_w[lo:hi, :]).then_inc(self.s_bl, 16)
        dma(self.stage_g[64:P, 1, :], gate_w[0:64, :]).then_inc(self.s_bl, 16)
        dma(self.stage_b[:, :], b1.rearrange("e (k p) -> (e k) p", p=P)).then_inc(self.s_bl, 16)
        dma(self.bias2[:, :, :], b2.rearrange("(a e) c -> a e c", a=1).to_broadcast([P, NE, C])).then_inc(self.s_bl, 16)
        dma(self.bias_g[:, :], gate_b.rearrange("(a e) -> a e", a=1).to_broadcast([P, NE])).then_inc(self.s_bl, 16)

    def load_expert(self, sp, e, w1, w2):
        for s, (lo, hi, at) in enumerate(((0, P, 0), (P, C, 0), (64, C, 0))):
            sp.dma_start(self.stage1[at:at + hi - lo, s, :], w1[e, lo:hi, :]).then_inc(self.s_load, 16)
        sp.dma_start(self.stage1[64:P, 1, :], w1[e, 0:64, :]).then_inc(self.s_load, 16)
        sp.dma_start(self.stage2[:, :, :], w2[e].rearrange("(k p) c -> p k c", p=P)).then_inc(self.s_load, 16)

    def split_piece(self, dve, e, i):
        w1, w2, a, b = self.w1, self.w2, self.stage1, self.stage2
        if i == 0:
            dve.wait_ge(self.s_load, 80 * (e + 1))
        if i < 2:
            dst, src = ((w1[:, e, 0:3, :], a[:, :, :]), (w2[:, e, 0, :, :], b[:, :, :]))[i]
            dve.tensor_scalar(dst, src, WSCALE, None, ALU.mult).then_inc(self.s_split, 1)
            return
        if i == 2:
            dve.wait_ge(self.s_split, WPIECES * e + 2)
        src, hi, lo = ((a[:, 0, :], w1[:, e, 0, :], w1[:, e, 3, :]),
                       (a[0:64, 1, :], w1[0:64, e, 1, :], w1[0:64, e, 4, :]),
                       (b[:, :, :], w2[:, e, 0, :, :], w2[:, e, 1, :, :]))[i - 2]
        dve.scalar_tensor_tensor(lo, src, WSCALE, hi, ALU.mult, ALU.subtract).then_inc(self.s_split, 1)


def post_order():
    out = []
    for r in range(NT + 2):
        out += [(k, r - lag) for lag, k in enumerate("abc") if 0 <= r - lag < NT]
    return out


X_UNITS = tuple(range(NT))
ROUNDS = tuple(range(13, 63, 5))
EARLY_POST = tuple(range(6, 12))
POST_SLOTS = [(3, 4)] * (NT - 1) + [(4,), (3, 4), (0,)]


def unit_jobs():
    post = iter(post_order())
    jobs = {u: [] for u in range(UNITS)}
    for t, u in enumerate(X_UNITS):
        jobs[u].append(("x", t))
    for u in EARLY_POST:
        jobs[u].append(next(post))
    jobs[ROUNDS[0] - 1].append(("n", 0))
    for r, u in enumerate(ROUNDS):
        if r < NT:
            jobs[u].append(("u", r))
            jobs[u + 1].append(("v", r))
        if r >= 2:
            jobs[u + 1].append(("q", r - 2))
            jobs[u + 3].append(("k", r - 2))
        if r + 1 < NT:
            jobs[u + 2].append(("n", r + 1))
        for v in POST_SLOTS[r]:
            jobs[u + v].append(next(post))
    assert next(post, None) is None and jobs[ROUNDS[NT + 1] + 3][-1] == ("k", NT - 1)
    return jobs


JOBS = unit_jobs()
PRE_STEPS = 63
POST_STEPS = NT


def has_pre(img):
    return not isinstance(img, int) or img + 1 < B


def has_post(img):
    return not isinstance(img, int) or img >= 1


def jobs_at(img, u):
    return [(k, t) for k, t in JOBS.get(u, []) if (has_post(img) if k in "abc" else has_pre(img))]


def jobs_of(img):
    return [j for u in range(UNITS) for j in jobs_at(img, u)]


def on_scalar(img, kind):
    if isinstance(img, int) and img == -1:
        return kind in "qkn"
    if isinstance(img, int) and img == B:
        return kind == "b"
    return kind in "qn"


def count(img, jobs, scalar=None):
    return sum(scalar is None or on_scalar(img, k) == scalar for k, _ in jobs)


def jobs_before(img, scalar=None):
    if isinstance(img, int) and img <= 1 or isinstance(img, int) and img == B:
        return sum(count(i, jobs_of(i), scalar) for i in range(-1, img))
    return jobs_before(1, scalar) + count(2, jobs_of(2), scalar) * (img - 1)


def attention_phase(nc, ctx, mlp, mlp_args, x, temp, qkv_w, qkv_b, proj_w, proj_b, x1_tokens):
    def sb(name, shape, dt=F32):
        return ctx.enter_context(nc.sbuf_tensor(name, shape, dt))

    def sem(name):
        return ctx.enter_context(nc.semaphore(name))

    x_img = x.rearrange("b (k c) h w -> b c k (h w)", k=2)
    x1_img = x1_tokens.rearrange("(b t p) c -> b p t c", p=P, t=NT)

    ident = sb("ident", [P, P])
    ident16 = sb("ident16", [P, P], F16)
    w_all = sb("w_all", [P, 5, WCOLS], F16)
    bias_qkv = sb("bias_qkv", [P, QKV])
    bias_proj = sb("bias_proj", [P, C])
    temps = sb("temps", [P, NH])
    shift = sb("shift", [P, 2, NH])
    x_in, x_tok = mlp.x_in, mlp.x_tok
    x_res = sb("x_res", [P, 2, NT, C])
    stats = sb("stats", [P, NT, 6])
    mean = sb("mean", [P, NT])
    var = sb("var", [P, NT])
    rstd = sb("rstd", [P, NT])
    tmp8 = sb("tmp8", [P, NT])
    xn = sb("xn", [P, C])
    xn_split = sb("xn_split", [P, 2, 2 * C], F16)
    xn_t = sb("xn_t", [P, 2, 3, P], F16)
    qk, qk_split = mlp.qk, mlp.qk_split
    qk_sq = sb("qk_sq", [P, 2 * NH, HD])
    sumsq = sb("sumsq", [P, NT, 2 * NH])
    inv_norm = sb("inv_norm", [P, NT, 2 * NH])
    minus_half = sb("minus_half", [P, 2 * NH])
    v_aug = sb("v_aug", [P, 2, NT, NH, 32])
    stacks = [mlp.stacks_even, sb("stacks_odd", [KROWS, 2, NH, NTOK], F16)]
    probs = sb("probs", [P, PRING, NTOK])
    o_sb = sb("o_sb", [P, 2, 2, NTOK])
    o_norm = sb("o_norm", [P, 2, C])
    o_rec = sb("o_rec", [P, NH])
    o_split = sb("o_split", [P, 2, 2 * C], F16)
    o_t = sb("o_t", [P, 2, 3, P], F16)
    x1 = sb("x1", [P, NT, C])
    flat = probs[:, :, :].rearrange("p r n -> p (r n)")
    nsrc = WJ * 2 * C
    w_src = flat[0:HC, 0:nsrc].rearrange("p (j c) -> p j c", j=WJ)
    w_f32 = flat[:, nsrc:nsrc + 3 * WCOLS].rearrange("p (s n) -> p s n", s=3)

    ps_s = ctx.enter_context(nc.psum_tensor("ps_s", [P, 2, 2, HALF], F32))
    ps_o = ctx.enter_context(nc.psum_tensor("ps_o", [P, 2, HALF], F32))
    ps_m = ctx.enter_context(nc.psum_tensor("ps_m", [P, 2, HALF], F32))

    s_const = sem("s_const")
    s_zero = sem("s_zero")
    s_x1_free = sem("s_x1_free")
    s_wload = sem("s_wload")
    s_bload = sem("s_bload")
    s_wt = sem("s_wt")
    s_wt_free = sem("s_wt_free")
    s_setup = sem("s_setup")
    s_x = sem("s_x")

    with nc.Block() as block:
        @block.sync
        def _(sp):
            wv = qkv_w.rearrange("(j r) c -> r j c", r=HC)
            wp = proj_w.rearrange("(j r) c -> r j c", r=HC)
            for lo in (0, C):
                sp.dma_start(w_src[:, 0:6, lo:lo + C], wv).then_inc(s_wload, 16)
                sp.dma_start(w_src[:, 6:WJ, lo:lo + C], wp).then_inc(s_wload, 16)
            sp.dma_start(x_in[:, :, :], x_img[0]).then_inc(s_x, 16)
            sp.dma_start(bias_qkv[:, :], qkv_b.rearrange("(a n) -> a n", a=1).to_broadcast([P, QKV])).then_inc(s_bload, 16)
            sp.dma_start(bias_proj[:, :], proj_b.rearrange("(a n) -> a n", a=1).to_broadcast([P, C])).then_inc(s_bload, 16)
            sp.dma_start(temps[:, :], temp.rearrange("h a b -> (a b) h").to_broadcast([P, NH])).then_inc(s_bload, 16)

        @block.scalar
        def _(act):
            gate_w, gate_b, w1, b1, w2, b2 = mlp_args
            mlp.load_small(act.dma_start, gate_w, gate_b, b1, b2)

        @block.gpsimd
        def _(pool):
            pool.memset(ident[:, :], 0.0).then_inc(s_zero, 1)
            pool.memset(ident16[:, :], 0.0).then_inc(s_zero, 1)
            pool.wait_ge(s_zero, 2)
            for m in (ident, ident16):
                pool.affine_select(out=m[:, :], in_=m[:, :], compare_op=ALU.not_equal, fill=1.0, base=0,
                                   pattern=[[-1, P]], channel_multiplier=1).then_inc(s_const, 1)
            own = Steps(pool, s_const, 2)
            own.now(pool.memset(v_aug[:, :, :, :, HD:HD + 1], 1.0 / OSCALE))
            own.now(pool.memset(v_aug[:, :, :, :, HD + 1:32], 0.0))
            pool.memset(x1[:, 0, 0:1], 0.0).then_inc(s_x1_free, 16)

        @block.tensor
        def _(pe):
            pe.wait_ge(s_const, 1)
            pe.wait_ge(s_wload, 64)
            n = 0
            for s, lo in ((0, 0), (1, P), (2, 64)):
                for j in range(WJ):
                    if n >= 2:
                        pe.wait_ge(s_wt_free, n - 1)
                    pe.transpose(ps_m[:, n % 2, 0:HC], w_src[:, j, lo:lo + P], ident[0:HC, 0:HC]).then_inc(s_wt, 1)
                    n += 1

        @block.vector
        def _(dve):
            st = Steps(dve, s_setup)
            n = 0
            for s in range(3):
                for j in range(WJ):
                    dve.wait_ge(s_wt, n + 1)
                    dve.tensor_scalar(w_f32[:, s, j * HC:(j + 1) * HC], ps_m[:, n % 2, 0:HC], WSCALE, None,
                                      ALU.mult).then_inc(s_wt_free, 1)
                    n += 1
            dve.wait_ge(s_wt_free, n)
            st.now(dve.tensor_copy(w_all[:, 0:3, :], w_f32))
            st.now(dve.tensor_tensor(w_all[:, 3, :], w_f32[:, 0, :], w_all[:, 0, :], ALU.subtract))
            st.now(dve.tensor_tensor(w_all[0:64, 4, :], w_f32[0:64, 1, :], w_all[0:64, 1, :], ALU.subtract))
            dve.wait_ge(s_bload, 48)
            st.now(dve.memset(minus_half[:, :], -0.5))
            st.now(dve.tensor_scalar(shift[:, 0, :], temps[:, :], -1.0, None, ALU.mult))
            st.now(dve.tensor_tensor(shift[:, 1, :], shift[:, 0, :], temps[:, :], ALU.max))
            st.now(dve.tensor_scalar(shift[:, 0, :], shift[:, 1, :], -EXP_RANGE, 0.0, ALU.add, ALU.max))
            st.now(dve.tensor_scalar(shift[:, 1, :], shift[:, 0, :], -1.0, None, ALU.mult))

    s_job = sem("s_job")
    s_job_done = sem("s_job_done")
    s_job_act = sem("s_job_act")
    s_xn = sem("s_xn")
    s_qk = sem("s_qk")
    s_scores = sem("s_scores")
    s_probs = sem("s_probs")
    s_pv = sem("s_pv")
    s_o = sem("s_o")
    s_pre = sem("s_pre")
    s_var = sem("s_var")
    s_rstd = sem("s_rstd")
    s_res = sem("s_res")
    s_sumsq = sem("s_sumsq")
    s_inv = sem("s_inv")
    s_post = sem("s_post")
    s_o_lo = sem("s_o_lo")

    def wait_taken(eng, img, job):
        n = job if isinstance(job, int) else jobs_of(img).index(job)
        if n < 0:
            img, n = img - 1, n + len(jobs_of(img - 1))
        scalar = on_scalar(img, jobs_of(img)[n][0])
        eng.wait_ge(s_job_act if scalar else s_job_done,
                    jobs_before(img, scalar) + count(img, jobs_of(img)[:n + 1], scalar))

    def job_bank(img, n):
        if isinstance(img, int) and img == B and n % 6 >= 2:
            return ps_s[:, (n % 6 - 2) // 2, n % 2, :]
        return ps_m[:, n % 2, :]

    def sp_image(sp, img):
        if not isinstance(img, int) or img + 2 < B:
            sp.wait_ge(s_job, jobs_before(img) + jobs_of(img).index(("x", NT - 1)) + 1)
            nxt = img + 2 if isinstance(img, int) else (img + 2) % B
            sp.dma_start(x_in[:, :, :], x_img[nxt]).then_inc(s_x, 16)
        if isinstance(img, int) and img == B - 1:
            sp.wait_ge(s_job, jobs_before(B - 1))
            sp.wait_ge(s_x, 16 * (B + 1))
            sp.wait_ge(s_xn, NT * B)
            sp.wait_ge(s_res, B)
            for e in range(NE):
                if e:
                    sp.wait_ge(mlp.s_split, WPIECES * e)
                mlp.load_expert(sp, e, mlp_args[2], mlp_args[4])
        if has_post(img):
            wait_taken(sp, img, ("c", NT - 1))
            sp.dma_start(x1_img[img - 1], x1[:, :, :]).then_inc(s_x1_free, 16)

    def scores(pe, img, par, u):
        g, m, j = u // (UNITS // 2), u % (UNITS // 2) // GH, u % GH
        h = g * GH + j
        if u == 0:
            last = jobs_of(img - 1)
            for kind in "qk":
                wait_taken(pe, img, last.index((kind, NT - 1)) - len(last))
        if not (isinstance(img, int) and UNITS * img + u < 2):
            pe.wait_ge(s_probs, UNITS * img + (u - 1))
        for f in range(2):
            mm = pe.matmul(ps_s[:, u % 2, f, :], stacks[par][:, 1, h, m * P:(m + 1) * P],
                           stacks[par][:, 0, h, f * HALF:(f + 1) * HALF], start=True, stop=True)
        mm.then_inc(s_scores, 1)

    def pv(pe, img, par, k):
        p, f = k // 2, k % 2
        g, m = p // (UNITS // 4), p % (UNITS // 4) // 2
        if f == 0:
            pe.wait_ge(s_probs, UNITS * img + 2 * p + 2)
        if p % (UNITS // 4) == 0 and not (isinstance(img, int) and img == 0 and g == 0):
            pe.wait_ge(s_o, 4 * img + 2 * g + f - 1)
        for u in (2 * p, 2 * p + 1):
            j = u % GH
            mm = pe.matmul(ps_o[32 * j:32 * j + 32, f, :], v_aug[:, par, m, g * GH + j, :],
                           probs[:, u % PRING, f * HALF:(f + 1) * HALF], start=(m == 0), stop=(m == NT - 1))
        mm.then_inc(s_pv, 1)

    def products(pe, out, rows_t, cols):
        for i, (c, w, rows) in enumerate(PRODUCTS):
            mm = pe.matmul(out, rows_t[0:rows, c, :], w_all[0:rows, w, cols], start=(i == 0), stop=(i == 4))
        return mm

    def pe_job(pe, img, par, n, job):
        kind, t = job
        bank = job_bank(img, n)
        if isinstance(img, int) and img == B and n == 2:
            pe.wait_ge(s_probs, UNITS * B)
        elif isinstance(img, int) and img == B and n > 2:
            if n >= 6:
                wait_taken(pe, img, n - 6)
        elif not (isinstance(img, int) and img == -1 and n < 2):
            wait_taken(pe, img, n - 2)
        tile = slice(t * P, (t + 1) * P)
        npre = NT * (img + 1)
        if kind == "x":
            if t == 0:
                pe.wait_ge(s_x, 16 * (img + 2))
            for k in range(2):
                mm = pe.transpose(bank[:, k * HC:(k + 1) * HC], x_in[:, k, tile], ident[0:HC, 0:HC])
        elif kind == "n":
            pe.wait_ge(s_xn, npre + t + 1)
            b16 = bank.bitcast(F16)
            for k in range(3):
                mm = pe.transpose(b16[:, k * P:(k + 1) * P], xn_split[:, t % 2, k * P:(k + 1) * P], ident16[:, :])
        elif kind in "uv":
            if kind == "u":
                wait_taken(pe, img, ("n", t))
            off = QCOLS * "uv".index(kind)
            mm = products(pe, bank[:, 0:QCOLS], xn_t[:, t % 2, :, :], slice(off, off + QCOLS))
        elif kind in "qk":
            if kind == "q":
                pe.wait_ge(s_qk, npre + t + 1)
            b16 = bank.bitcast(F16)
            for h in range(NH):
                mm = pe.transpose(b16[0:4 * HD, h * P:(h + 1) * P],
                                  qk_split[:, t % QRING, NH * "qk".index(kind) + h, :, :].rearrange("p a d -> p (a d)"),
                                  ident16[:, :])
        elif kind == "a":
            if t == 0:
                pe.wait_ge(s_o, 4 * img)
            for g in range(2):
                mm = pe.transpose(bank[:, g * P:(g + 1) * P], o_sb[:, 1 - par, g, tile], ident[:, :])
        elif kind == "b":
            pe.wait_ge(s_o_lo, NT * (img - 1) + t + 1)
            b16 = bank.bitcast(F16)
            for k in range(3):
                mm = pe.transpose(b16[:, k * P:(k + 1) * P], o_split[:, t % 2, k * P:(k + 1) * P], ident16[:, :])
        else:
            wait_taken(pe, img, ("b", t))
            mm = products(pe, bank[:, 0:C], o_t[:, t % 2, :, :], slice(QKV, WCOLS))
        mm.then_inc(s_job, 1)

    def pe_image(pe, img, par, attend=True):
        n = 0
        for u in range(UNITS):
            if attend:
                scores(pe, img, par, u)
            if u >= 3 and attend:
                pv(pe, img, par, u - 3)
            elif u < 3 and has_post(img):
                pv(pe, img - 1, 1 - par, UNITS - 3 + u)
            for job in jobs_at(img, u):
                pe_job(pe, img, par, n, job)
                n += 1

    def act_image(act, img, par, attend=True):
        n = 0
        for u in range(UNITS):
            if attend:
                act.wait_ge(s_scores, UNITS * img + u + 1)
                if not (isinstance(img, int) and UNITS * img + u < PRING):
                    act.wait_ge(s_pv, UNITS * img + 2 * ((u - PRING) // 2) + 2)
                h = u // (UNITS // 2) * GH + u % GH
                act.activation(probs[:, u % PRING, :], ps_s[:, u % 2, :, :].rearrange("p f n -> p (f n)"),
                               ACT.Exp, bias=shift[:, 1, h:h + 1], scale=temps[:, h:h + 1]).then_inc(s_probs, 1)
            for kind, t in jobs_at(img, u):
                scalar, bank = on_scalar(img, kind), job_bank(img, n)
                if scalar:
                    act.wait_ge(s_job, jobs_before(img) + n + 1)
                if scalar and kind in "nb":
                    act.activation((xn_t if kind == "n" else o_t)[:, t % 2, :, :].rearrange("p k n -> p (k n)"),
                                   bank.bitcast(F16)[:, 0:3 * P], ACT.Copy).then_inc(s_job_act, 1)
                elif scalar:
                    act.activation(stacks[1 - par][:, "qk".index(kind), :, t * P:(t + 1) * P],
                                   bank.bitcast(F16)[0:KROWS, :].rearrange("p (h n) -> p h n", h=NH),
                                   ACT.Copy).then_inc(s_job_act, 1)
                n += 1

    def take_o(dve, img, par, g, f):
        dve.wait_ge(s_pv, UNITS * img + UNITS // 2 * (g + 1) - 1 + f)
        dve.tensor_copy(o_sb[:, par, g, f * HALF:(f + 1) * HALF], ps_o[:, f, :]).then_inc(s_o, 1)

    def dve_job(dve, img, par, n, job, pre, post):
        kind, t = job
        done = jobs_before(img, False) + count(img, jobs_of(img)[:n], False)
        bank = job_bank(img, n)
        dve.wait_ge(s_job, jobs_before(img) + n + 1)
        if not (isinstance(img, int) and img == -1 and n == 0):
            dve.wait_ge(s_job_done, done)
        nxt = 1 - par
        if kind == "x":
            if t == 0 and not (isinstance(img, int) and img == -1):
                dve.wait_ge(s_res, img + 1)
            dve.bn_stats(stats[:, t, :], bank[:, 0:C])
            dve.tensor_copy(x_tok[:, t, :], bank[:, 0:C]).then_inc(s_job_done, 1)
        elif kind == "u":
            dve.scalar_tensor_tensor(qk[:, t, :, :].rearrange("p h d -> p (h d)")[:, 0:QCOLS], bank[:, 0:QCOLS],
                                     1.0 / WSCALE, bias_qkv[:, 0:QCOLS], ALU.mult, ALU.add).then_inc(s_job_done, 1)
        elif kind == "v":
            dve.scalar_tensor_tensor(v_aug[:, nxt, t, :, 0:HD], bank[:, HC:HC + C].rearrange("p (h d) -> p h d", d=HD),
                                     1.0 / WSCALE, bias_qkv[:, 2 * C:QKV].rearrange("p (h d) -> p h d", d=HD),
                                     ALU.mult, ALU.add)
            dve.scalar_tensor_tensor(qk[:, t, :, :].rearrange("p h d -> p (h d)")[:, QCOLS:2 * C], bank[:, 0:HC],
                                     1.0 / WSCALE, bias_qkv[:, QCOLS:2 * C], ALU.mult, ALU.add).then_inc(s_job_done, 1)
        elif kind in "qk":
            dve.tensor_copy(stacks[nxt][:, "qk".index(kind), :, t * P:(t + 1) * P],
                            bank.bitcast(F16)[0:KROWS, :].rearrange("p (h n) -> p h n", h=NH)).then_inc(s_job_done, 1)
        elif kind == "a":
            o = bank[:, 0:2 * P].rearrange("p (h d) -> p h d", d=32)
            post.now(dve.reciprocal(o_rec[:, :], o[:, :, HD]))
            if t >= 2:
                dve.wait_ge(s_o_lo, NT * (img - 1) + t - 1)
            elif not (isinstance(img, int) and img == 1):
                dve.wait_ge(s_o_lo, NT * (img - 1))
            rec = o_rec[:, :].unsqueeze(2).to_broadcast([P, NH, HD])
            hi = o_split[:, t % 2, 0:C]
            dve.tensor_tensor(o_norm[:, t % 2, :].rearrange("p (h d) -> p h d", d=HD), o[:, :, 0:HD], rec, ALU.mult)
            dve.tensor_tensor(hi.rearrange("p (h d) -> p h d", d=HD), o[:, :, 0:HD], rec,
                              ALU.mult).then_inc(s_job_done, 1)
        elif kind == "b":
            dve.tensor_copy(o_t[:, t % 2, :, :].rearrange("p k n -> p (k n)"),
                            bank.bitcast(F16)[:, 0:3 * P]).then_inc(s_job_done, 1)
        else:
            if t == 0:
                dve.wait_ge(s_x1_free, 16 * img)
                if not has_pre(img):
                    dve.wait_ge(s_res, img)
            dve.scalar_tensor_tensor(x1[:, t, :], bank[:, 0:C], 1.0 / (WSCALE * OSCALE), x_res[:, nxt, t, :],
                                     ALU.mult, ALU.add).then_inc(s_job_done, 1)

    def split_rows(dve, img, t, pre):
        if t == 0:
            dve.wait_ge(s_rstd, img + 2)
        else:
            dve.wait_ge(s_xn, NT * (img + 1) + t)
        if t >= 2:
            wait_taken(dve, img, ("n", t - 2))
        pre.now(dve.tensor_scalar(xn[:, :], x_tok[:, t, :], mean[:, t:t + 1], rstd[:, t:t + 1],
                                  ALU.subtract, ALU.mult))
        pre.now(dve.tensor_copy(xn_split[:, t % 2, 0:C], xn[:, :]))
        dve.tensor_tensor(xn_split[:, t % 2, C:2 * C], xn[:, :], xn_split[:, t % 2, 0:C],
                          ALU.subtract).then_inc(s_xn, 1)

    def head_norms(dve, img, t, pre):
        wait_taken(dve, img, ("v", t))
        if not (isinstance(img, int) and img == -1 and t == 0):
            dve.wait_ge(s_sumsq, NT * (img + 1) + t)
        pre.now(dve.tensor_tensor(qk_sq[:, :, :], qk[:, t, :, :], qk[:, t, :, :], ALU.mult))
        dve.tensor_reduce(sumsq[:, t, :], qk_sq[:, :, :], AX.X, ALU.add).then_inc(s_sumsq, 1)

    def split_heads(dve, img, t, pre, part):
        q2, k2 = (qk[:, t, NH * i:NH * (i + 1), :].unsqueeze(2).to_broadcast([P, NH, 2, HD]) for i in range(2))
        qs, ks = (qk_split[:, t % QRING, NH * i:NH * (i + 1), :, :] for i in range(2))
        if part == 0:
            dve.wait_ge(s_inv, NT * (img + 1) + t + 1)
            pre.now(dve.scalar_tensor_tensor(qk[:, t, :, :],
                                             inv_norm[:, t, :].unsqueeze(2).to_broadcast([P, 2 * NH, HD]),
                                             1.0 / NORM_EPS, qk[:, t, :, :], ALU.min, ALU.mult))
        elif part == 1:
            if t >= QRING:
                wait_taken(dve, img, ("k", t - QRING))
            pre.mark(dve.tensor_copy(qs[:, :, 0:4:2, :], q2))
            pre.now(dve.tensor_copy(ks[:, :, 0:2, :], k2))
            pre.mark(dve.tensor_tensor(qs[:, :, 1:4:2, :], q2, qs[:, :, 0:4:2, :], ALU.subtract))
        else:
            dve.tensor_tensor(ks[:, :, 2:4, :], k2, ks[:, :, 0:2, :], ALU.subtract).then_inc(s_qk, 1)

    def pool_image(pool, img, par):
        for u in range(UNITS):
            if has_pre(img) and u == X_UNITS[-1] + 1:
                pool.wait_ge(s_var, img + 2)
                pool.tensor_tensor(rstd[:, :], var[:, :], minus_half[:, 0:NT], ALU.pow).then_inc(s_rstd, 1)
            for kind, t in jobs_at(img, u):
                if kind == "a":
                    wait_taken(pool, img, ("a", t))
                    pool.tensor_tensor(o_split[:, t % 2, C:2 * C], o_norm[:, t % 2, :], o_split[:, t % 2, 0:C],
                                       ALU.subtract).then_inc(s_o_lo, 1)
            if has_pre(img) and u - 1 in ROUNDS[:NT]:
                t = ROUNDS.index(u - 1)
                pool.wait_ge(s_sumsq, NT * (img + 1) + t + 1)
                pool.tensor_tensor(inv_norm[:, t, :], sumsq[:, t, :], minus_half[:, :], ALU.pow).then_inc(s_inv, 1)
        if not has_pre(img):
            return
        if has_post(img):
            wait_taken(pool, img, ("c", NT - 1))
        else:
            wait_taken(pool, img, ("x", NT - 1))
        pool.tensor_tensor(x_res[:, 1 - par, :, :], x_tok[:, :, :],
                           bias_proj[:, :].unsqueeze(1).to_broadcast([P, NT, C]), ALU.add).then_inc(s_res, 1)

    def dve_image(dve, img, par, attend=True):
        n = 0
        pre = Steps(dve, s_pre, PRE_STEPS * (img + 1))
        post = Steps(dve, s_post, POST_STEPS * (img - 1))
        if has_pre(img) and not (isinstance(img, int) and img == -1):
            dve.wait_ge(s_xn, NT * (img + 1))
            dve.wait_ge(s_qk, NT * (img + 1))
        for u in range(UNITS):
            if u in (1, 2) and has_post(img):
                take_o(dve, img - 1, 1 - par, 1, u - 1)
            if u in (33, 34) and attend:
                take_o(dve, img, par, 0, u - 33)
            for job in jobs_at(img, u):
                if not on_scalar(img, job[0]):
                    dve_job(dve, img, par, n, job, pre, post)
                n += 1
            if isinstance(img, int) and img == B - 1 and WUNIT <= u and (u % WUNIT) < WPIECES and u // WUNIT <= NE:
                if u == WUNIT:
                    dve.wait_ge(s_probs, UNITS * (B - 1))
                    dve.wait_ge(s_sumsq, NT * B)
                    dve.wait_ge(s_qk, NT * B)
                    dve.wait_ge(s_job, jobs_before(B - 1))
                mlp.split_piece(dve, u // WUNIT - 1, u % WUNIT)
            if has_pre(img):
                if u == X_UNITS[-1] + 1:
                    wait_taken(dve, img, ("x", NT - 1))
                    mean_and_var(dve, pre, stats, mean[:, :], var[:, :], tmp8[:, :], LN1_EPS, s_var)
                if u == ROUNDS[0] - 2:
                    for t in range(2):
                        split_rows(dve, img, t, pre)
                r = sum(first <= u for first in ROUNDS) - 1
                v = u - ROUNDS[r]
                if v == 1 and 0 <= r < NT:
                    head_norms(dve, img, r, pre)
                if v in (0, 2, 3) and 0 < r <= NT:
                    split_heads(dve, img, r - 1, pre, (0, 2, 3).index(v))
                if v == 4 and 0 <= r and r + 2 < NT:
                    split_rows(dve, img, r + 2, pre)
        if has_post(img):
            assert post.n == POST_STEPS, post.n
        if has_pre(img):
            assert pre.n == PRE_STEPS, (pre.n, PRE_STEPS)

    with nc.Block() as block:
        @block.sync
        def _(sp):
            sp_image(sp, -1)
            sp_image(sp, 0)
            with sp.Fori(0, B // 2 - 1) as i:
                for k in range(2):
                    sp_image(sp, i * 2 + 1 + k)
            sp_image(sp, B - 1)
            sp_image(sp, B)
            sp.wait_ge(s_x1_free, 16 * (B + 1))

        @block.tensor
        def _(pe):
            pe_image(pe, -1, 1, attend=False)
            pe_image(pe, 0, 0)
            with pe.Fori(0, B // 2 - 1) as i:
                for k in range(2):
                    pe_image(pe, i * 2 + 1 + k, 1 - k)
            pe_image(pe, B - 1, 1)
            pe_image(pe, B, 0, attend=False)

        @block.scalar
        def _(act):
            act_image(act, -1, 1, attend=False)
            act_image(act, 0, 0)
            with act.Fori(0, B // 2 - 1) as i:
                for k in range(2):
                    act_image(act, i * 2 + 1 + k, 1 - k)
            act_image(act, B - 1, 1)
            act_image(act, B, 0, attend=False)

        @block.gpsimd
        def _(pool):
            pool_image(pool, -1, 1)
            pool_image(pool, 0, 0)
            with pool.Fori(0, B // 2 - 1) as i:
                for k in range(2):
                    pool_image(pool, i * 2 + 1 + k, 1 - k)
            pool_image(pool, B - 1, 1)
            pool_image(pool, B, 0)

        @block.vector
        def _(dve):
            dve_image(dve, -1, 1, attend=False)
            dve_image(dve, 0, 0)
            with dve.Fori(0, B // 2 - 1) as i:
                for k in range(2):
                    dve_image(dve, i * 2 + 1 + k, 1 - k)
            dve_image(dve, B - 1, 1)
            dve_image(dve, B, 0, attend=False)


BT = 4
BTOK = BT * P
NBLK = B * NTOK // BTOK
STEPS = NE * NK
LAG = 2
HBUF, HSPLIT = 3, 4
MLP_PRE_STEPS = 59
F_AT, N_AT, G_AT = 4, 11, 15
EXP_AT, GATE_AT = 16, 17


def mlp_jobs_at(blk, n):
    post = not isinstance(blk, int) or blk >= 1
    pre = not isinstance(blk, int) or blk + 1 < NBLK
    jobs = []
    if post and F_AT <= n < F_AT + BT:
        jobs.append(("f", n - F_AT))
    if pre and N_AT <= n < N_AT + BT:
        jobs.append(("n", n - N_AT))
    if pre and n == G_AT:
        jobs.append(("g", 0))
    return jobs


def mlp_job_base(blk):
    if isinstance(blk, int) and blk <= 0:
        return (BT + 1) * (blk + 1)
    if isinstance(blk, int) and blk == NBLK:
        return mlp_job_base(blk - 1) + BT
    return 2 * (BT + 1) + (2 * BT + 1) * (blk - 1)


def mlp_phase(nc, ctx, mlp, x1_tokens, out):
    def sb(name, shape, dt=F32):
        return ctx.enter_context(nc.sbuf_tensor(name, shape, dt))

    def sem(name):
        return ctx.enter_context(nc.semaphore(name))

    x1_blk = x1_tokens.rearrange("(q t p) c -> q p t c", p=P, t=BT)
    out_img = out.rearrange("b (k c) h w -> b c k (h w)", k=2)

    ident = sb("m_ident", [P, P])
    ident16 = sb("m_ident16", [P, P], F16)
    w1_sb, w2_sb = mlp.w1, mlp.w2
    wg_sb = sb("wg_sb", [P, 5, NE], F16)
    bias1 = sb("bias1", [P, NE * NK])
    bias2, bias_g, stage_g, stage_b = mlp.bias2, mlp.bias_g, mlp.stage_g, mlp.stage_b
    lower = sb("lower", [P, NE, NE])
    x1_in = sb("x1_in", [P, BT, C])
    stats = sb("m_stats", [P, BT, 6])
    mean = sb("m_mean", [P, BT])
    var = sb("m_var", [P, BT])
    rstd = sb("m_rstd", [P, BT])
    tmp4 = sb("m_tmp4", [P, BT])
    xn = sb("m_xn", [P, BT, C])
    xn_split = sb("m_xn_split", [P, BT, 2 * C], F16)
    xn_t = sb("m_xn_t", [P, 2, 3, BTOK], F16)
    h_f32 = sb("h_f32", [P, HBUF, BTOK])
    h_split = sb("h_split", [P, HSPLIT, 2, BTOK], F16)
    acc = sb("acc", [P, 2, BT, C])
    logits = sb("logits", [P, BT, NE])
    top = sb("top", [P, BT])
    expo = sb("expo", [P, BT, NE])
    prob = sb("prob", [P, BT, NE])
    beats = sb("beats", [P, BT, NE, NE])
    ties = sb("ties", [P, BT, NE, NE])
    rank = sb("rank", [P, BT, NE])
    total = sb("total", [P, BT])
    gates = sb("gates", [P, 2, BT, NE])
    gates_w = sb("gates_w", [P, 2, BT, NE])
    y_out = sb("y_out", [HC, 2, BTOK])

    ps_h = ctx.enter_context(nc.psum_tensor("ps_h", [P, HBUF, BTOK], F32))
    ps_y = ctx.enter_context(nc.psum_tensor("ps_y", [P, 2, 2, 512], F32))
    ps_j = ctx.enter_context(nc.psum_tensor("ps_j", [P, 512], F32))

    s_zero, s_const = sem("m_zero"), sem("m_const")
    s_bl = mlp.s_bl
    s_b1 = sem("m_b1")
    s_hi = sem("m_hi")
    s_x1 = sem("m_x1")
    s_setup = sem("m_setup")
    s_out = sem("m_out")

    gate_parts = [(stage_g[:, 0, :], wg_sb[:, 0, :], wg_sb[:, 3, :]),
                  (stage_g[0:64, 1, :], wg_sb[0:64, 1, :], wg_sb[0:64, 4, :])]

    with nc.Block() as block:
        @block.sync
        def _(sp):
            sp.dma_start(x1_in[:, :, :], x1_blk[0]).then_inc(s_x1, 16)

        @block.scalar
        def _(act):
            act.wait_ge(s_bl, 16 * 7)
            act.activation(wg_sb[:, 0:3, :], stage_g[:, :, :], ACT.Copy, scale=WSCALE).then_inc(s_hi, 1)

        @block.gpsimd
        def _(pool):
            pool.memset(ident[:, :], 0.0).then_inc(s_zero, 1)
            pool.memset(ident16[:, :], 0.0).then_inc(s_zero, 1)
            pool.memset(lower[:, :, :], 0.0).then_inc(s_zero, 1)
            pool.wait_ge(s_zero, 3)
            for m in (ident, ident16):
                pool.affine_select(out=m[:, :], in_=m[:, :], compare_op=ALU.not_equal, fill=1.0, base=0,
                                   pattern=[[-1, P]], channel_multiplier=1).then_inc(s_const, 1)
            own = Steps(pool, s_const, 2)
            for i in range(1, NE):
                own.now(pool.memset(lower[:, i, 0:i], 1.0))
            pool.memset(y_out[:, 0, 0:1], 0.0).then_inc(s_out, 16)

        @block.tensor
        def _(pe):
            pe.wait_ge(s_const, 1)
            pe.wait_ge(s_bl, 16 * 7)
            pe.transpose(ps_j[:, 0:NE * NK], stage_b[:, :], ident[0:NE * NK, 0:NE * NK]).then_inc(s_b1, 1)

        @block.vector
        def _(dve):
            st = Steps(dve, s_setup)

            dve.wait_ge(s_hi, 1)
            for a, hi, lo in gate_parts:
                st.mark(dve.scalar_tensor_tensor(lo, a, WSCALE, hi, ALU.mult, ALU.subtract))
            dve.wait_ge(s_b1, 1)
            dve.tensor_copy(bias1[:, :], ps_j[:, 0:NE * NK])

    s_job = sem("m_job")
    s_job_done = sem("m_job_done")
    s_xn = sem("m_xn")
    s_w1 = sem("m_h")
    s_gelu = sem("m_gelu")
    s_h = sem("m_hsplit")
    s_w2 = sem("m_y")
    s_acc = sem("m_acc")
    s_logit = sem("m_logit")
    s_exp = sem("m_exp")
    s_acc0 = sem("m_acc0")
    s_pre = sem("m_pre")
    s_own = sem("m_own")

    def first(blk):
        return isinstance(blk, int) and blk == -1

    def sp_block(sp, blk, img, half):
        if not isinstance(blk, int) or blk >= 1:
            sp.wait_ge(s_job_done, mlp_job_base(blk) + BT)
            sp.dma_start(out_img[img][:, :, half * BTOK:(half + 1) * BTOK], y_out[:, :, :]).then_inc(s_out, 16)
        if not isinstance(blk, int) or blk + 2 < NBLK:
            nxt = blk + 2 if isinstance(blk, int) else (blk + 2) % NBLK
            sp.wait_ge(s_acc0, blk + 2)
            sp.dma_start(x1_in[:, :, :], x1_blk[nxt]).then_inc(s_x1, 16)

    def first_product(pe, blk, par, n):
        e, k = n // NK, n % NK
        if n == 0:
            pe.wait_ge(s_job_done, mlp_job_base(blk))
        if not (isinstance(blk, int) and STEPS * blk + n < HBUF):
            pe.wait_ge(s_gelu, STEPS * blk + n - HBUF + 1)
        for i, (c, w, rows) in enumerate(PRODUCTS):
            mm = pe.matmul(ps_h[:, n % HBUF, :], w1_sb[0:rows, e, w, k * P:(k + 1) * P], xn_t[0:rows, par, c, :],
                           start=(i == 0), stop=(i == 4))
        mm.then_inc(s_w1, 1)

    def second_product(pe, blk, n):
        e, k = n // NK, n % NK
        pe.wait_ge(s_h, STEPS * blk + n + 1)
        if k == 0 and not (isinstance(blk, int) and NE * blk + e < 2):
            pe.wait_ge(s_acc, NE * blk + e - 1)
        for t in range(BT):
            y = ps_y[:, e % 2, t // 2, (t % 2) * C:(t % 2 + 1) * C]
            tok = slice(t * P, (t + 1) * P)
            for i, (hp, wp) in enumerate(((0, 0), (0, 1), (1, 0))):
                mm = pe.matmul(y, h_split[:, n % HSPLIT, hp, tok], w2_sb[:, e, wp, k, :],
                               start=(k == 0 and i == 0 and t % 2 == 0), stop=(k == NK - 1 and i == 2),
                               skip_group_check=True)
        mm.then_inc(s_w2, 1)

    def pe_mlp_job(pe, blk, par, base, j, job):
        kind, t = job
        if not (first(blk) and j == 0):
            pe.wait_ge(s_job_done, base + j)
        if kind == "f":
            if t == 0:
                pe.wait_ge(s_acc, NE * blk)
            for k in range(2):
                mm = pe.transpose(ps_j[0:HC, k * P:(k + 1) * P], acc[:, 1 - par, t, k * HC:(k + 1) * HC], ident[:, :])
        elif kind == "n":
            if t == 0:
                pe.wait_ge(s_xn, blk + 2)
            b16 = ps_j[:, :].bitcast(F16)
            for k in range(3):
                mm = pe.transpose(b16[:, k * P:(k + 1) * P], xn_split[:, t, k * P:(k + 1) * P], ident16[:, :])
        else:
            for t in range(BT):
                for i, (c, w, rows) in enumerate(PRODUCTS):
                    mm = pe.matmul(ps_j[:, t * NE:(t + 1) * NE], xn_t[0:rows, 1 - par, c, t * P:(t + 1) * P],
                                   wg_sb[0:rows, w, :], start=(i == 0), stop=(i == 4))
        mm.then_inc(s_job, 1)

    def pe_block(pe, blk, par, main=True):
        base, j = mlp_job_base(blk), 0
        for n in range(STEPS):
            if main:
                first_product(pe, blk, par, n)
            if n >= LAG and main:
                second_product(pe, blk, n - LAG)
            elif n < LAG and (not isinstance(blk, int) or blk >= 1):
                second_product(pe, blk - 1, STEPS - LAG + n)
            for job in mlp_jobs_at(blk, n):
                pe_mlp_job(pe, blk, par, base, j, job)
                j += 1

    def act_block(act, blk, main=True):
        for n in range(STEPS):
            if main:
                act.wait_ge(s_w1, STEPS * blk + n + 1)
                if not (isinstance(blk, int) and STEPS * blk + n < HSPLIT):
                    act.wait_ge(s_w2, STEPS * blk + n - HSPLIT + 1)
                act.activation(h_split[:, n % HSPLIT, 0, :], ps_h[:, n % HBUF, :], ACT.Gelu, bias=bias1[:, n:n + 1],
                               scale=1.0 / WSCALE)
                if not (isinstance(blk, int) and STEPS * blk + n < HBUF):
                    act.wait_ge(s_h, STEPS * blk + n - HBUF + 1)
                act.activation(h_f32[:, n % HBUF, :], ps_h[:, n % HBUF, :], ACT.Gelu, bias=bias1[:, n:n + 1],
                               scale=1.0 / WSCALE).then_inc(s_gelu, 1)
            if n == EXP_AT and (not isinstance(blk, int) or blk + 1 < NBLK):
                act.wait_ge(s_logit, blk + 2)
                act.activation(expo[:, :, :], logits[:, :, :], ACT.Exp).then_inc(s_exp, 1)

    def pool_block(pool, blk):
        for n in range(STEPS):
            pool.wait_ge(s_gelu, STEPS * blk + n + 1)
            if not (isinstance(blk, int) and STEPS * blk + n < HSPLIT):
                pool.wait_ge(s_w2, STEPS * blk + n - HSPLIT + 1)
            pool.tensor_tensor(h_split[:, n % HSPLIT, 1, :], h_f32[:, n % HBUF, :], h_split[:, n % HSPLIT, 0, :],
                               ALU.subtract).then_inc(s_h, 1)

    def add_expert(dve, blk, par, e, own):
        dve.wait_ge(s_w2, STEPS * blk + (e + 1) * NK)
        for t in range(BT):
            ins = dve.scalar_tensor_tensor(acc[:, par, t, :], ps_y[:, e % 2, t // 2, (t % 2) * C:(t % 2 + 1) * C],
                                           gates_w[:, par, t, e:e + 1], acc[:, par, t, :], ALU.mult, ALU.add)
            if t < BT - 1:
                own.mark(ins)
        ins.then_inc(s_acc, 1)
        dve.wait_ge(s_acc, NE * blk + e + 1)

    def mlp_dve_job(dve, blk, par, base, j, job, pre):
        kind, t = job
        dve.wait_ge(s_job, base + j + 1)
        if not (first(blk) and j == 0):
            dve.wait_ge(s_job_done, base + j)
        if kind == "f":
            if t == 0:
                dve.wait_ge(s_out, 16 * blk)
            dve.tensor_copy(y_out[:, :, t * P:(t + 1) * P],
                            ps_j[0:HC, 0:2 * P].rearrange("p (k n) -> p k n", k=2)).then_inc(s_job_done, 1)
        elif kind == "n":
            dve.tensor_copy(xn_t[:, 1 - par, :, t * P:(t + 1) * P],
                            ps_j[:, :].bitcast(F16)[:, 0:3 * P].rearrange("p (k n) -> p k n", k=3)).then_inc(s_job_done, 1)
        else:
            dve.scalar_tensor_tensor(logits[:, :, :], ps_j[:, 0:BT * NE].rearrange("p (t e) -> p t e", e=NE),
                                     1.0 / WSCALE, bias_g[:, :].unsqueeze(1).to_broadcast([P, BT, NE]),
                                     ALU.mult, ALU.add).then_inc(s_job_done, 1)
            dve.wait_ge(s_job_done, base + j + 1)
            pre.now(dve.tensor_reduce(top[:, :], logits[:, :, :], AX.X, ALU.max))
            dve.tensor_tensor(logits[:, :, :], logits[:, :, :], top[:, :].unsqueeze(2).to_broadcast([P, BT, NE]),
                              ALU.subtract).then_inc(s_logit, 1)

    def gate_weights(dve, blk, nxt, pre):
        dve.wait_ge(s_exp, blk + 2)
        dve.wait_ge(s_logit, blk + 2)
        bc = lambda v: v.unsqueeze(2).to_broadcast([P, BT, NE])
        pre.now(dve.tensor_reduce(total[:, :], expo[:, :, :], AX.X, ALU.add))
        pre.now(dve.reciprocal(total[:, :], total[:, :]))
        pre.now(dve.tensor_tensor(prob[:, :, :], expo[:, :, :], bc(total[:, :]), ALU.mult))
        p_i = prob[:, :, :].unsqueeze(3).to_broadcast([P, BT, NE, NE])
        p_j = prob[:, :, :].unsqueeze(2).to_broadcast([P, BT, NE, NE])
        pre.mark(dve.tensor_tensor(beats[:, :, :, :], p_j, p_i, ALU.is_gt))
        pre.now(dve.tensor_tensor(ties[:, :, :, :], p_j, p_i, ALU.is_equal))
        pre.now(dve.tensor_tensor(ties[:, :, :, :], ties[:, :, :, :],
                                  lower[:, :, :].unsqueeze(1).to_broadcast([P, BT, NE, NE]), ALU.mult))
        pre.now(dve.tensor_tensor(beats[:, :, :, :], beats[:, :, :, :], ties[:, :, :, :], ALU.add))
        pre.now(dve.tensor_reduce(rank[:, :, :], beats[:, :, :, :], AX.X, ALU.add))
        pre.now(dve.tensor_scalar(rank[:, :, :], rank[:, :, :], 2.0, None, ALU.is_lt))
        pre.now(dve.tensor_tensor(prob[:, :, :], prob[:, :, :], rank[:, :, :], ALU.mult))
        pre.now(dve.tensor_reduce(total[:, :], prob[:, :, :], AX.X, ALU.add))
        pre.now(dve.tensor_scalar(total[:, :], total[:, :], 1e-9, None, ALU.add))
        pre.now(dve.reciprocal(total[:, :], total[:, :]))
        pre.now(dve.tensor_tensor(gates[:, nxt, :, :], prob[:, :, :], bc(total[:, :]), ALU.mult))
        pre.now(dve.tensor_scalar(gates_w[:, nxt, :, :], gates[:, nxt, :, :], 1.0 / WSCALE, None, ALU.mult))

    def start_acc(dve, blk, nxt, t, pre):
        src = x1_in[:, t, :]
        for e in range(NE):
            ins = dve.scalar_tensor_tensor(acc[:, nxt, t, :], bias2[:, e, :], gates[:, nxt, t, e:e + 1], src,
                                           ALU.mult, ALU.add)
            src = acc[:, nxt, t, :]
            if t < BT - 1 or e < NE - 1:
                pre.now(ins)
        if t == BT - 1:
            ins.then_inc(s_acc0, 1)
            dve.wait_ge(s_acc0, blk + 2)

    def dve_block(dve, blk, par, main=True):
        base, j = mlp_job_base(blk), 0
        has_pre = not isinstance(blk, int) or blk + 1 < NBLK
        has_post = not isinstance(blk, int) or blk >= 1
        nxt = 1 - par
        pre = Steps(dve, s_pre, MLP_PRE_STEPS * (blk + 1))
        own = Steps(dve, s_own, NE * (BT - 1) * blk)
        if has_post:
            own.base = own.base - (BT - 1)
        for n in range(STEPS):
            if n == 2 and has_post:
                add_expert(dve, blk - 1, nxt, NE - 1, own)
            if main and n in (8, 14, 20):
                add_expert(dve, blk, par, (n - 8) // NK, own)
            if has_pre:
                if n == 3:
                    dve.wait_ge(s_x1, 16 * (blk + 2))
                    for t in range(BT):
                        pre.mark(dve.bn_stats(stats[:, t, :], x1_in[:, t, :]))
                    pre.wait(pre.n)
                if n == 4:
                    mean_and_var(dve, pre, stats, mean[:, :], var[:, :], tmp4[:, :], LN2_EPS)
                if n in (5, 6, 7):
                    rsqrt(dve, pre, var[:, :], rstd[:, :], tmp4[:, :], n - 5)
                if n == 8:
                    if not first(blk):
                        dve.wait_ge(s_xn, blk + 1)
                    for t in range(BT):
                        pre.mark(dve.tensor_scalar(xn[:, t, :], x1_in[:, t, :], mean[:, t:t + 1],
                                                   rstd[:, t:t + 1], ALU.subtract, ALU.mult))
                    pre.wait(pre.n)
                if n == 9:
                    pre.now(dve.tensor_copy(xn_split[:, :, 0:C], xn[:, :, :]))
                if n == 10:
                    dve.tensor_tensor(xn_split[:, :, C:2 * C], xn[:, :, :], xn_split[:, :, 0:C],
                                      ALU.subtract).then_inc(s_xn, 1)
            for job in mlp_jobs_at(blk, n):
                mlp_dve_job(dve, blk, par, base, j, job, pre)
                j += 1
            if has_pre:
                if n == GATE_AT:
                    gate_weights(dve, blk, nxt, pre)
                if n in (18, 19, 21, 22):
                    start_acc(dve, blk, nxt, (18, 19, 21, 22).index(n), pre)
        if has_pre:
            assert pre.n == MLP_PRE_STEPS, pre.n

    with nc.Block() as block:
        @block.sync
        def _(sp):
            sp_block(sp, -1, 0, 0)
            sp_block(sp, 0, 0, 0)
            with sp.Fori(0, NBLK // 2 - 1) as i:
                for k in range(2):
                    sp_block(sp, i * 2 + 1 + k, i, k)
            sp_block(sp, NBLK - 1, B - 1, 0)
            sp_block(sp, NBLK, B - 1, 1)
            sp.wait_ge(s_out, 16 * (NBLK + 1))

        @block.tensor
        def _(pe):
            pe_block(pe, -1, 1, main=False)
            pe_block(pe, 0, 0)
            with pe.Fori(0, NBLK // 2 - 1) as i:
                for k in range(2):
                    pe_block(pe, i * 2 + 1 + k, 1 - k)
            pe_block(pe, NBLK - 1, 1)
            pe_block(pe, NBLK, 0, main=False)

        @block.scalar
        def _(act):
            act_block(act, -1, main=False)
            act_block(act, 0)
            with act.Fori(0, NBLK // 2 - 1) as i:
                for k in range(2):
                    act_block(act, i * 2 + 1 + k)
            act_block(act, NBLK - 1)

        @block.gpsimd
        def _(pool):
            pool_block(pool, 0)
            with pool.Fori(0, NBLK // 2 - 1) as i:
                for k in range(2):
                    pool_block(pool, i * 2 + 1 + k)
            pool_block(pool, NBLK - 1)

        @block.vector
        def _(dve):
            dve_block(dve, -1, 1, main=False)
            dve_block(dve, 0, 0)
            with dve.Fori(0, NBLK // 2 - 1) as i:
                for k in range(2):
                    dve_block(dve, i * 2 + 1 + k, 1 - k)
            dve_block(dve, NBLK - 1, 1)
            dve_block(dve, NBLK, 0, main=False)


_INS = ['x', 'L0_conv_temperature', 'L0_conv_qkv_w', 'L0_conv_qkv_b', 'L0_conv_proj_w', 'L0_conv_proj_b',
        'L0_ffn_gate_w', 'L0_ffn_gate_b', 'L0_ffn_w1', 'L0_ffn_b1', 'L0_ffn_w2', 'L0_ffn_b2']
_OUTS = [((B, C, 32, 32), 'float32')]


def metaformer_block(nc, x, temp, qkv_w, qkv_b, proj_w, proj_b, gate_w, gate_b, w1, b1, w2, b2, out, x1_tokens=None):
    if x1_tokens is None:
        x1_tokens = nc.dram_tensor("x1_tokens", [B * NTOK, C], F32, kind="Internal").ap()
    mlp_args = (gate_w, gate_b, w1, b1, w2, b2)
    with ExitStack() as both:
        mlp = Mlp(nc, both)
        with ExitStack() as ctx:
            attention_phase(nc, ctx, mlp, mlp_args, x, temp, qkv_w, qkv_b, proj_w, proj_b, x1_tokens)
        with ExitStack() as ctx:
            mlp_phase(nc, ctx, mlp, x1_tokens, out)


def kernel(**inputs):
    import numpy as _np
    import concourse.bacc as _bacc
    from concourse.bass_utils import run_bass_kernel_spmd as _run

    nc = _bacc.Bacc("TRN2", target_bir_lowering=False, num_devices=1)
    arrays, args = {}, []
    for name in _INS:
        a = _np.ascontiguousarray(inputs[name])
        arrays[f"in_{name}_dram"] = a
        args.append(nc.dram_tensor(f"in_{name}_dram", a.shape, mybir.dt.from_np(a.dtype), kind="ExternalInput").ap())
    for i, (shape, dtype) in enumerate(_OUTS):
        dt = mybir.dt.from_np(_np.dtype(dtype))
        args.append(nc.dram_tensor(f"out_{i}_dram", shape, dt, kind="ExternalOutput").ap())
    metaformer_block(nc, *args)
    r = _run(nc, [arrays], core_ids=[0])
    return r.results[0]["out_0_dram"]
```
